# Optimizing a Trainium2 kernel written in Bass

```python
import numpy as np
import jax
import jax.numpy as jnp

def _softmax(x, axis=-1):
    return jax.nn.softmax(x, axis=axis)

def _gelu(x):
    return jax.nn.gelu(x, approximate=True)

def _silu(x):
    return jax.nn.silu(x)

def _sigmoid(x):
    return jax.nn.sigmoid(x)

def _layernorm(x, axis=-1, eps=1e-05):
    m = jnp.mean(x, axis=axis, keepdims=True)
    v = jnp.var(x, axis=axis, keepdims=True)
    return (x - m) / jnp.sqrt(v + eps)

def _scatter_add(tgt, idx, src, axis=0):
    return tgt.at[idx].add(src)

def _segment_sum(src, seg, n):
    return jax.ops.segment_sum(src, seg, n)
kernel_name = 'mk_adj_ffn_d2_adj_r2_865f39'

def setup_inputs(seed: int=0):
    np.random.seed(seed)
    _w = jnp.asarray

    def _rec_inputs():
        import jax
        import jax.numpy as jnp
        _gk = jax.random.key(seed)
        x = -0.0002928 + 1 * jax.random.normal(jax.random.fold_in(_gk, 1), (32, 256, 128), jnp.float32)
        _a = jax.random.bernoulli(jax.random.fold_in(_gk, 2), 0.03125, (256, 256))
        _a = jnp.logical_or(_a, jnp.swapaxes(_a, -1, -2))
        _a = jnp.logical_or(_a, jnp.eye(256, dtype=bool))
        adj = _a.astype(jnp.int32)
        return (x, adj)
    x, adj = _rec_inputs()

    def _L0_gnn_setup():
        import jax, jax.numpy as jnp
        import numpy as np
        ALPHA = 0.2
        key = jax.random.key(seed)
        k1, k2, k3, k4 = jax.random.split(key, 4)
        B, N, Din, Dout = (8, 1024, 128, 128)
        h = jax.random.normal(k1, (B, N, Din), dtype=jnp.float32)
        adj = jax.random.randint(k2, (N, N), 0, 2, dtype=jnp.int32)
        w_bound = float(np.sqrt(6.0 / (Din + Dout)))
        a_bound = float(np.sqrt(6.0 / (2 * Dout + 1)))
        W = jax.random.uniform(k3, (Din, Dout), dtype=jnp.float32, minval=-w_bound, maxval=w_bound)
        a = jax.random.uniform(k4, (2 * Dout, 1), dtype=jnp.float32, minval=-a_bound, maxval=a_bound)
        return {'h': h, 'adj': adj, 'W': W, 'a': a}
    _L0_gnn_all = _L0_gnn_setup()
    _L0_gnn_in = {k: v for k, v in _L0_gnn_all.items() if k in ('W', 'a')}
    del _L0_gnn_all

    def _L0_ffn_setup():
        import jax, jax.numpy as jnp
        import numpy as np
        D_MODEL = 128
        N_EXPERTS = 16
        HIDDEN = 256
        SCALE = 0.02
        key = jax.random.key(seed)
        ks = jax.random.split(key, 5)
        x = jax.random.normal(ks[0], (4, 4096, D_MODEL), dtype=jnp.float32)
        gate_w = jax.random.normal(ks[1], (D_MODEL, N_EXPERTS), dtype=jnp.float32) * SCALE
        gate_b = jnp.zeros((N_EXPERTS,), dtype=jnp.float32)
        w1 = jax.random.normal(ks[2], (N_EXPERTS, D_MODEL, HIDDEN), dtype=jnp.float32) * SCALE
        w2 = jax.random.normal(ks[3], (N_EXPERTS, D_MODEL, HIDDEN), dtype=jnp.float32) * SCALE
        w3 = jax.random.normal(ks[4], (N_EXPERTS, HIDDEN, D_MODEL), dtype=jnp.float32) * SCALE
        return {'x': x, 'gate_w': gate_w, 'gate_b': gate_b, 'w1': w1, 'w2': w2, 'w3': w3}
    _L0_ffn_all = _L0_ffn_setup()
    _L0_ffn_in = {k: v for k, v in _L0_ffn_all.items() if k in ('gate_w', 'gate_b', 'w1', 'w2', 'w3')}
    del _L0_ffn_all

    def _L1_gnn_setup():
        import jax, jax.numpy as jnp
        import numpy as np
        NEG_BIG = -9000000000000000.0
        key = jax.random.key(seed)
        k1, k2, k3, k4 = jax.random.split(key, 4)
        bs, N, Fin, Fout = (8, 1024, 128, 128)
        x = jax.random.normal(k1, (bs, N, Fin), dtype=jnp.float32)
        adj = jax.random.randint(k2, (N, N), 0, 2, dtype=jnp.int32)
        W = jax.random.normal(k3, (Fin, Fout), dtype=jnp.float32) * (1.414 / np.sqrt(Fin))
        a = jax.random.normal(k4, (2 * Fout, 1), dtype=jnp.float32) * 0.1
        return {'x': x, 'adj': adj, 'W': W, 'a': a}
    _L1_gnn_all = _L1_gnn_setup()
    _L1_gnn_in = {k: v for k, v in _L1_gnn_all.items() if k in ('W', 'a')}
    del _L1_gnn_all

    def _L1_ffn_setup():
        import jax, jax.numpy as jnp
        import numpy as np
        DIM = 128
        HEADS = 8
        NUM_KEYS = 128
        NUM_KV = NUM_KEYS ** 2
        PK_TOPK = 16
        FINAL_TOPK = 16
        DIM_KEY = DIM // 2
        P = 2

        def _pk(x, Wq_pk, pk_keys):
            b, n, _ = x.shape
            q = (x @ Wq_pk).reshape(b, n, P, HEADS, DIM_KEY).transpose(2, 0, 1, 3, 4)
            sim = jnp.einsum('pbnhd,pkhd->pbnhk', q, pk_keys)
            scores, idx = jax.lax.top_k(sim, PK_TOPK)
            idx0 = idx[0]
            idx1 = idx[1] * NUM_KEYS
            index = (idx0[..., :, None] + idx1[..., None, :]).reshape(b, n, HEADS, PK_TOPK * PK_TOPK)
            score = (scores[0][..., :, None] + scores[1][..., None, :]).reshape(b, n, HEADS, PK_TOPK * PK_TOPK)
            final_scores, pk_idx = jax.lax.top_k(score, FINAL_TOPK)
            final_indices = jnp.take_along_axis(index, pk_idx, axis=-1)
            final_scores = jax.nn.softmax(final_scores, axis=-1)
            return (final_scores, final_indices)
        key = jax.random.key(seed)
        ks = jax.random.split(key, 7)
        b, n = (2, 512)
        std = 0.02
        x = jax.random.normal(ks[0], (b, n, DIM), dtype=jnp.float32)
        Wq_pk = jax.random.normal(ks[1], (DIM, P * HEADS * DIM_KEY), dtype=jnp.float32) * std
        pk_keys = jax.random.normal(ks[2], (P, NUM_KEYS, HEADS, DIM_KEY), dtype=jnp.float32) * std
        Wq = jax.random.normal(ks[3], (DIM, HEADS * DIM), dtype=jnp.float32) * std
        keys_table = jax.random.normal(ks[4], (NUM_KV * HEADS, DIM), dtype=jnp.float32) * std
        values_table = jax.random.normal(ks[5], (NUM_KV * HEADS, DIM), dtype=jnp.float32) * std
        Wo = jax.random.normal(ks[6], (DIM * HEADS, DIM), dtype=jnp.float32) * std
        return {'x': x, 'Wq_pk': Wq_pk, 'pk_keys': pk_keys, 'Wq': Wq, 'keys_table': keys_table, 'values_table': values_table, 'Wo': Wo}
    _L1_ffn_all = _L1_ffn_setup()
    _L1_ffn_in = {k: v for k, v in _L1_ffn_all.items() if k in ('Wq_pk', 'pk_keys', 'Wq', 'keys_table', 'values_table', 'Wo')}
    del _L1_ffn_all
    return {'x': x, 'adj': adj, 'L0_gnn_W': _L0_gnn_in['W'], 'L0_gnn_a': _L0_gnn_in['a'], 'L0_ffn_gate_w': _L0_ffn_in['gate_w'], 'L0_ffn_gate_b': _L0_ffn_in['gate_b'], 'L0_ffn_w1': _L0_ffn_in['w1'], 'L0_ffn_w2': _L0_ffn_in['w2'], 'L0_ffn_w3': _L0_ffn_in['w3'], 'L1_gnn_W': _L1_gnn_in['W'], 'L1_gnn_a': _L1_gnn_in['a'], 'L1_ffn_Wq_pk': _L1_ffn_in['Wq_pk'], 'L1_ffn_pk_keys': _L1_ffn_in['pk_keys'], 'L1_ffn_Wq': _L1_ffn_in['Wq'], 'L1_ffn_keys_table': _L1_ffn_in['keys_table'], 'L1_ffn_values_table': _L1_ffn_in['values_table'], 'L1_ffn_Wo': _L1_ffn_in['Wo']}

def reference(x, adj, L0_gnn_W, L0_gnn_a, L0_ffn_gate_w, L0_ffn_gate_b, L0_ffn_w1, L0_ffn_w2, L0_ffn_w3, L1_gnn_W, L1_gnn_a, L1_ffn_Wq_pk, L1_ffn_pk_keys, L1_ffn_Wq, L1_ffn_keys_table, L1_ffn_values_table, L1_ffn_Wo):
    import jax
    import jax.numpy as jnp

    def _L0_gnn_ref(h, adj, W, a):
        import jax, jax.numpy as jnp
        import numpy as np
        ALPHA = 0.2
        Wh = jnp.matmul(h, W)
        D = W.shape[1]
        e_src = jnp.matmul(Wh, a[:D])
        e_dst = jnp.matmul(Wh, a[D:])
        e = e_src + jnp.swapaxes(e_dst, 1, 2)
        e = jnp.where(e > 0, e, ALPHA * e)
        mask = (adj > 0)[None, :, :]
        e = jnp.where(mask, e, -jnp.inf)
        alpha_w = jax.nn.softmax(e, axis=-1)
        h_prime = jnp.matmul(alpha_w, Wh)
        return jax.nn.elu(h_prime)

    def _L0_ffn_ref(x, gate_w, gate_b, w1, w2, w3):
        import jax, jax.numpy as jnp
        import numpy as np
        D_MODEL = 128
        N_EXPERTS = 16
        HIDDEN = 256
        SCALE = 0.02
        n_experts = w1.shape[0]
        logits = jnp.einsum('bsd,de->bse', x, gate_w) + gate_b
        probs = jax.nn.softmax(logits, axis=-1)
        top_probs, top_idx = jax.lax.top_k(probs, 2)
        top_probs = top_probs / jnp.sum(top_probs, axis=-1, keepdims=True)
        dispatch = jnp.sum(jax.nn.one_hot(top_idx, n_experts, dtype=x.dtype) * top_probs[..., None], axis=-2)
        h1 = jnp.einsum('bsd,edh->bseh', x, w1)
        h2 = jnp.einsum('bsd,edh->bseh', x, w2)
        hidden = jax.nn.silu(h1) * h2
        expert_out = jnp.einsum('bseh,eho->bseo', hidden, w3)
        return jnp.einsum('bseo,bse->bso', expert_out, dispatch)

    def _L1_gnn_ref(x, adj, W, a):
        import jax, jax.numpy as jnp
        import numpy as np
        NEG_BIG = -9000000000000000.0
        alpha = 0.2
        h = jnp.matmul(x, W)
        Fout = h.shape[-1]
        a1, a2 = (a[:Fout, 0], a[Fout:, 0])
        s1 = jnp.einsum('bnf,f->bn', h, a1)
        s2 = jnp.einsum('bnf,f->bn', h, a2)
        e = jax.nn.leaky_relu(s1[:, :, None] + s2[:, None, :], negative_slope=alpha)
        attention = jnp.where(adj[None, :, :] > 0, e, NEG_BIG)
        attention = jax.nn.softmax(attention, axis=-1)
        h_prime = jnp.matmul(attention, h)
        return jax.nn.elu(h_prime)

    def _L1_ffn_ref(x, Wq_pk, pk_keys, Wq, keys_table, values_table, Wo):
        import jax, jax.numpy as jnp
        import numpy as np
        DIM = 128
        HEADS = 8
        NUM_KEYS = 128
        NUM_KV = NUM_KEYS ** 2
        PK_TOPK = 16
        FINAL_TOPK = 16
        DIM_KEY = DIM // 2
        P = 2

        def _pk(x, Wq_pk, pk_keys):
            b, n, _ = x.shape
            q = (x @ Wq_pk).reshape(b, n, P, HEADS, DIM_KEY).transpose(2, 0, 1, 3, 4)
            sim = jnp.einsum('pbnhd,pkhd->pbnhk', q, pk_keys)
            scores, idx = jax.lax.top_k(sim, PK_TOPK)
            idx0 = idx[0]
            idx1 = idx[1] * NUM_KEYS
            index = (idx0[..., :, None] + idx1[..., None, :]).reshape(b, n, HEADS, PK_TOPK * PK_TOPK)
            score = (scores[0][..., :, None] + scores[1][..., None, :]).reshape(b, n, HEADS, PK_TOPK * PK_TOPK)
            final_scores, pk_idx = jax.lax.top_k(score, FINAL_TOPK)
            final_indices = jnp.take_along_axis(index, pk_idx, axis=-1)
            final_scores = jax.nn.softmax(final_scores, axis=-1)
            return (final_scores, final_indices)
        b, n, d = x.shape
        q = (x @ Wq).reshape(b, n, HEADS, DIM) * DIM ** (-0.5)
        kv_scores, indices = _pk(x, Wq_pk, pk_keys)
        offsets = jnp.arange(HEADS, dtype=indices.dtype) * NUM_KV
        ind = indices + offsets[None, None, :, None]
        k = jnp.einsum('bnhk,bnhkd->bnhd', kv_scores, keys_table[ind])
        v = jnp.einsum('bnhk,bnhkd->bnhd', kv_scores, values_table[ind])
        sim = jnp.einsum('bihd,bjhd->bhij', q, k)
        neg = -jnp.finfo(sim.dtype).max
        causal = jnp.tril(jnp.ones((n, n), dtype=bool))
        sim = jnp.where(causal, sim, neg)
        attn = jax.nn.softmax(sim, axis=-1)
        out = jnp.einsum('bhij,bjhd->bhid', attn, v)
        out = out.transpose(0, 2, 1, 3).reshape(b, n, HEADS * DIM)
        return out @ Wo
    x = x + _L0_gnn_ref(_layernorm(x, axis=-1), adj, L0_gnn_W, L0_gnn_a)
    x = x + _L0_ffn_ref(_layernorm(x, axis=-1), L0_ffn_gate_w, L0_ffn_gate_b, L0_ffn_w1, L0_ffn_w2, L0_ffn_w3)
    x = x + _L1_gnn_ref(_layernorm(x, axis=-1), adj, L1_gnn_W, L1_gnn_a)
    x = x + _L1_ffn_ref(_layernorm(x, axis=-1), L1_ffn_Wq_pk, L1_ffn_pk_keys, L1_ffn_Wq, L1_ffn_keys_table, L1_ffn_values_table, L1_ffn_Wo)
    return x

_drawn_inputs = setup_inputs


def setup_inputs(seed=0):
    import zlib

    import numpy as np

    out = dict(_drawn_inputs(seed))
    spreads = {'L0_ffn_gate_b': (0.0, 0.8)}
    factors = {'L0_ffn_gate_w': 8.0,
     'L0_ffn_w1': 8.0,
     'L0_ffn_w2': 8.0,
     'L0_ffn_w3': 8.0,
     'L1_ffn_Wq_pk': 47.744,
     'L1_ffn_pk_keys': 47.404,
     'L1_ffn_Wq': 64.0,
     'L1_ffn_keys_table': 64.0,
     'L1_ffn_values_table': 46.953,
     'L1_ffn_Wo': 46.837}
    for name, (base, spread) in spreads.items():
        noise = np.random.default_rng([zlib.crc32(name.encode()), seed]).standard_normal(out[name].shape)
        drawn = base * np.exp(spread * noise) if base else spread * noise
        out[name] = jnp.asarray(drawn.astype(out[name].dtype))
    for name, factor in factors.items():
        out[name] = (out[name] * factor).astype(out[name].dtype)
    return out
```

```python
from contextlib import ExitStack

import numpy as np

import concourse.bass as bass
from concourse import mybir

F32 = mybir.dt.float32
U32 = mybir.dt.uint32
I32 = mybir.dt.int32
ALU = mybir.AluOpType
ACT = mybir.ActivationFunctionType
AX = mybir.AxisListType

P = 128
D = 128
TOKENS = 256
TILES = TOKENS // P
EXPERTS = 16
HIDDEN = 256
CHUNKS = HIDDEN // P
HEADS = 8
KEYS = 128
DK = D // 2
TOPK = 16
STEPS = HEADS * TILES
SLOTS = 4
EPS = 1e-5
SLOPE = 0.2
NEG_BIG = -9e15
LOWEST = -3.0e38
RSQRT_MAGIC = 0x5F3759DF

PAIR_ROWS = [TOPK // (i + 1) for i in range(TOPK)]
PAIR_AT = [sum(PAIR_ROWS[:i]) for i in range(TOPK)]
PAIRS = sum(PAIR_ROWS)
SINGLES = PAIR_ROWS.index(1)

C_IDENT = 0
C_CAUSAL = C_IDENT + P
C_IOTA = C_CAUSAL + 2 * P
C_HEAD = C_IOTA + PAIRS
C_ALL = C_HEAD + HEADS * TOPK


def shape_constants():
    c = np.zeros((P, C_ALL), np.float32)
    c[:, C_IDENT:C_IDENT + P] = np.eye(P)
    i = np.arange(P)
    c[:, C_CAUSAL + P:C_CAUSAL + 2 * P] = np.where(i[None, :] <= i[:, None], 0.0, LOWEST)
    c[:, C_IOTA:C_IOTA + PAIRS] = np.arange(PAIRS)
    c[:, C_HEAD:C_HEAD + HEADS * TOPK] = np.repeat(np.arange(HEADS) * KEYS * KEYS, TOPK)
    return c


def build(nc, x, adj, consts, gat_w, gat_wt, gat_a, gate_w, gate_b, w1, w2, w3, pk_wt, pk_kt, wq, table, wo, out):
    BATCHES = x.shape[0]

    with ExitStack() as ctx:
        def sb(name, shape, dt=F32):
            return ctx.enter_context(nc.sbuf_tensor(name, shape, dt))

        def ps(name):
            return ctx.enter_context(nc.psum_tensor(name, [P, 512], F32))

        sems = []

        def sem(name):
            s = ctx.enter_context(nc.semaphore(name))
            sems.append(s)
            return s

        const = sb("const", [P, C_ALL])
        ident = const[:, C_IDENT:C_IDENT + P]
        causal = const[:, C_CAUSAL:C_CAUSAL + 2 * P]
        iota = const[:, C_IOTA:C_IOTA + PAIRS]
        head_row = const[:, C_HEAD:C_HEAD + HEADS * TOPK]
        w1_sb = sb("w1_sb", [P, EXPERTS, HIDDEN])
        w2_sb = sb("w2_sb", [P, EXPERTS, HIDDEN])
        w3_sb = sb("w3_sb", [P, EXPERTS * CHUNKS, D])
        gate_w_sb = sb("gate_w_sb", [P, EXPERTS])
        gate_b_sb = sb("gate_b_sb", [P, EXPERTS])
        wq_sb = sb("wq_sb", [P, HEADS * D])
        wo_sb = sb("wo_sb", [P, HEADS, D])
        gat_ext = sb("gat_ext", [P, 2, D + 1])
        gat_dst = sb("gat_dst", [P, 2, P])
        adj_bias = sb("adj_bias", [P, TILES, TOKENS])
        pk_mat = sb("pk_mat", [P, HEADS * 2 * KEYS])

        res = sb("res", [P, TILES, D])
        stats = sb("stats", [P, TILES, 6])
        meanvar = sb("meanvar", [P, TILES, 2])
        rs_i = sb("rs_i", [P, TILES], I32)
        rs_y = sb("rs_y", [P, TILES])
        rs_t = sb("rs_t", [P, TILES])
        var_eps = sb("var_eps", [P, TILES])
        normed = sb("normed", [P, TILES, D])
        xT = sb("xT", [P, TOKENS])
        gat_h = sb("gat_h", [P, TILES, D + 1])
        edge = sb("edge", [P, TILES, TOKENS])
        edge_l = sb("edge_l", [P, TILES, TOKENS])
        edge_m = sb("edge_m", [P, TILES, TOKENS])
        edge_max = sb("edge_max", [P, TILES])
        edge_nmax = sb("edge_nmax", [P, TILES])
        edge_sum = sb("edge_sum", [P, TILES])
        edge_inv = sb("edge_inv", [P, TILES])
        edge_T = sb("edge_T", [P, 2 * TOKENS])
        elu_neg = sb("elu_neg", [P, TILES, D])
        elu_exp = sb("elu_exp", [P, TILES, D])
        elu_pos = sb("elu_pos", [P, TILES, D])
        logits = sb("logits", [P, TILES, EXPERTS])
        best = sb("best", [P, TILES, 8])
        best_i = sb("best_i", [P, TILES, 8], U32)
        best_f = sb("best_f", [P, TILES, 2])
        gap = sb("gap", [P, TILES])
        gap_exp = sb("gap_exp", [P, TILES])
        gate_den = sb("gate_den", [P, TILES])
        gate_p = sb("gate_p", [P, TILES, 2])
        disp = sb("disp", [P, TILES, 2, EXPERTS])
        dispatch = sb("dispatch", [P, TILES, EXPERTS])
        tanh_h = sb("tanh_h", [P, 2, 512])
        silu_h = sb("silu_h", [P, 2, 512])
        hid = sb("hid", [P, 2, CHUNKS, TOKENS])
        rest = sb("rest", [P, 2, KEYS])
        sc = sb("sc", [P, HEADS, 2, TOPK])
        ix = sb("ix", [P, HEADS, 2, TOPK], U32)
        ixf = sb("ixf", [P, HEADS, 2, TOPK])
        pair_s = sb("pair_s", [P, HEADS, PAIRS])
        pair_i = sb("pair_i", [P, HEADS, PAIRS])
        rest2 = sb("rest2", [P, 2, PAIRS])
        fin_s = sb("fin_s", [P, HEADS, TOPK])
        fin_p = sb("fin_p", [P, HEADS, TOPK], U32)
        fin_pf = sb("fin_pf", [P, HEADS, TOPK])
        hit = sb("hit", [P, 2, TOPK, PAIRS])
        fin_i = sb("fin_i", [P, HEADS, TOPK])
        fin_e = sb("fin_e", [P, HEADS, TOPK])
        fin_sum = sb("fin_sum", [P, HEADS])
        row_next = sb("row_next", [P, TILES, HEADS, TOPK], U32)
        wt_next = sb("wt_next", [P, TILES, HEADS, TOPK])

        row = sb("row", [P, TILES, HEADS, TOPK], U32)
        wt = sb("wt", [P, TILES, HEADS, TOPK])
        xT_cur = sb("xT_cur", [P, TOKENS])
        res_cur = sb("res_cur", [P, TILES, D])
        rows = sb("rows", [P, SLOTS, TOPK, 2 * D])
        part = sb("part", [P, 2 * D])
        kv = sb("kv", [P, 2, TILES, 2 * D])
        qk_sb = sb("qk_sb", [P, 2 * TOKENS])
        sim = sb("sim", [P, 3 * P])
        sim_max = sb("sim_max", [P, TILES])
        sim_nmax = sb("sim_nmax", [P, TILES])
        sim_sum = sb("sim_sum", [P, TILES])
        sim_inv = sb("sim_inv", [P, TILES])
        prob = sb("prob", [P, 3 * P])
        prob_T = sb("prob_T", [P, 3 * P])
        att_T = sb("att_T", [P, HEADS, TOKENS])
        y_sb = sb("y_sb", [P, TILES, D])

        f0, f1, f2, f3, f4 = (ps(f"front{i}") for i in range(5))
        p_qk, p_sim, p_tr = ps("p_qk"), ps("p_sim"), ps("p_tr")

        loaded = sem("loaded")
        ext_psum = sem("ext_psum")
        setup_mat = sem("setup_mat")
        setup_mat_sb = sem("setup_mat_sb")
        dve_step = sem("dve_step")
        act_step = sem("act_step")
        x_loaded = sem("x_loaded")
        handed_rows = sem("handed_rows")
        handed = sem("handed")
        normed_up = sem("normed_up")
        xT_psum = sem("xT_psum")
        xT_up = sem("xT_up")
        gat_psum = sem("gat_psum")
        gat_h_up = sem("gat_h_up")
        edge_up = sem("edge_up")
        nmax_up = sem("nmax_up")
        edge_exp = sem("edge_exp")
        edge_T_psum = sem("edge_T_psum")
        edge_T_up = sem("edge_T_up")
        gat_out = sem("gat_out")
        elu_in = sem("elu_in")
        elu_up = sem("elu_up")
        logits_psum = sem("logits_psum")
        gap_up = sem("gap_up")
        gap_exp_up = sem("gap_exp_up")
        h1_psum = sem("h1_psum")
        h2_psum = sem("h2_psum")
        tanh_up = sem("tanh_up")
        hid_up = sem("hid_up")
        moe_psum = sem("moe_psum")
        moe_added = sem("moe_added")
        scores_psum = sem("scores_psum")
        scores_read = sem("scores_read")
        fin_up = sem("fin_up")
        fin_exp = sem("fin_exp")
        fetched = [sem(f"fetched{i}") for i in range(SLOTS)]
        slot_free = sem("slot_free")
        qk_psum = sem("qk_psum")
        qk_up = sem("qk_up")
        sim_psum = sem("sim_psum")
        sim_nmax_up = sem("sim_nmax_up")
        sim_exp = sem("sim_exp")
        prob_up = sem("prob_up")
        prob_T_psum = sem("prob_T_psum")
        prob_T_up = sem("prob_T_up")
        att_psum = sem("att_psum")
        att_up = sem("att_up")
        y_psum = sem("y_psum")
        y_up = sem("y_up")
        y_stored = sem("y_stored")

        def clear_semaphores():
            for s in sems:
                nc.sync.sem_clear(s)
            nc.all_engine_barrier()

        pk_wt_sb = rows[0:DK, 0, :, :].rearrange("p a b -> p (a b)")[:, 0:2 * HEADS * D]
        pk_kt_sb = rows[0:DK, 0, :, :].rearrange("p a b -> p (a b)")[:, 2 * HEADS * D:4 * HEADS * D]
        adj_i = rows[:, 1, 0:2, :].bitcast(I32)
        gat_wt_sb = rows[:, 2, 0, :].rearrange("p (l e) -> p l e", l=2)
        gat_a_sb = rows[:, 2, 1, 0:4].rearrange("p (l e) -> p l e", l=2)

        with nc.Block() as block:
            @block.sync
            def _(sp):
                loads = [
                    (const[:, :], consts), (gat_wt_sb, gat_wt), (gat_a_sb, gat_a), (gat_ext[:, :, 0:D], gat_w),
                    (adj_i, adj.rearrange("(t p) j -> p t j", p=P)),
                    (pk_wt_sb, pk_wt), (pk_kt_sb, pk_kt),
                    (gate_w_sb[:, :], gate_w), (gate_b_sb[:, :], gate_b),
                    (w1_sb[:, :, :], w1.rearrange("e d h -> d e h")),
                    (w2_sb[:, :, :], w2.rearrange("e d h -> d e h")),
                    (w3_sb[:, :, :], w3.rearrange("e (c p) o -> p (e c) o", p=P)),
                    (wq_sb[:, :], wq), (wo_sb[:, :, :], wo.rearrange("(h d) n -> d h n", d=D)),
                ]
                for to, of in loads:
                    sp.dma_start(to, of).then_inc(loaded, 16)
                sp.wait_ge(loaded, 16 * len(loads))

            LOADS = 14

            @block.tensor
            def _(pe):
                pe.wait_ge(loaded, 16 * LOADS)
                for layer in range(2):
                    mm = nc.tensor.matmul(f0[:, 2 * layer:2 * layer + 2], gat_wt_sb[:, layer, :],
                                          gat_a_sb[:, layer, :], start=True, stop=True)
                mm.then_inc(ext_psum, 1)
                for n in range(2 * HEADS):
                    bank = (f1, f2)[n // 4 % 2]
                    if n % 4 == 0 and n >= 8:
                        pe.wait_ge(setup_mat_sb, n // 4 - 1)
                    mm = nc.tensor.matmul(bank[:, n % 4 * KEYS:(n % 4 + 1) * KEYS], pk_wt_sb[:, n * D:(n + 1) * D],
                                          pk_kt_sb[:, n * KEYS:(n + 1) * KEYS], start=True, stop=True)
                    if n % 4 == 3:
                        mm.then_inc(setup_mat, 1)

            @block.scalar
            def _(act):
                for c in range(2 * HEADS // 4):
                    act.wait_ge(setup_mat, c + 1)
                    nc.scalar.copy(pk_mat[:, 512 * c:512 * (c + 1)], (f1, f2)[c % 2][:, :]).then_inc(setup_mat_sb, 1)

            @block.vector
            def _(dve):
                dve.wait_ge(loaded, 16 * LOADS)
                nc.vector.tensor_scalar(adj_bias[:, :, :], adj_i, 0.0, None, ALU.is_gt).then_inc(dve_step, 1)
                dve.wait_ge(dve_step, 1)
                nc.vector.tensor_scalar(adj_bias[:, :, :], adj_bias[:, :, :], 1.0, -NEG_BIG, ALU.subtract,
                                        ALU.mult)
                nc.vector.memset(gat_dst[:, :, :], 1.0).then_inc(dve_step, 1)
                dve.wait_ge(dve_step, 2)
                dve.wait_ge(ext_psum, 1)
                for layer in range(2):
                    nc.vector.tensor_copy(gat_ext[:, layer, D:D + 1], f0[:, 2 * layer:2 * layer + 1])
                    nc.vector.tensor_scalar(gat_dst[:, layer, :], gat_dst[:, layer, :],
                                            f0[:, 2 * layer + 1:2 * layer + 2], None, ALU.mult)
        clear_semaphores()

        def front_parts(s):
            if s < 0:
                return []
            parts = {0: ["norm0"], 1: ["gat_a0"], 2: ["gat_b0"], 3: ["gat_c0", "norm1", "gate"],
                     4: ["moe0"], 5: ["moe1"], 6: ["moe2"], 7: ["moe3"],
                     8: ["norm2", "gat_a1"], 9: ["gat_b1"], 10: ["gat_c1", "norm3"],
                     11: ["keys0"], 12: ["keys1"], 13: ["keys2"], 14: ["keys3"]}
            return parts.get(s, [])

        def run_pass(b, front, gather, tail):
            heads_done = [HEADS - 1] * tail
            turns = []
            if tail:
                turns.append(("tail", HEADS - 1))
            nth = {}
            order = ([HEADS - 1] if tail else []) + (list(range(HEADS - 1)) if gather else [])
            for n, h in enumerate(order):
                nth[h] = n
            n_steps = STEPS

            with nc.Block() as block:
                @block.sync
                def _(sp):
                    if front:
                        if gather:
                            sp.wait_ge(handed, 1)
                        nxt = b + 1 if gather else b
                        sp.dma_start(res[:, :, :], x[nxt].rearrange("(t p) d -> p t d", p=P)).then_inc(x_loaded, 16)
                        sp.wait_ge(x_loaded, 16)
                    if tail:
                        sp.wait_ge(y_up, 1)
                        prev = b - 1
                        sp.dma_start(out[prev].rearrange("(t p) d -> p t d", p=P), y_sb[:, :, :]).then_inc(y_stored, 16)
                        sp.wait_ge(y_stored, 16)

                @block.gpsimd
                def _(pool):
                    if not gather:
                        return
                    pool.wait_ge(handed_rows, 1)
                    for s in range(STEPS):
                        h, t = s // TILES, s % TILES
                        before = s - SLOTS + (1 if tail else 0)
                        if s >= SLOTS or (tail and s == SLOTS - 1):
                            pool.wait_ge(slot_free, before + 1)
                        for k in range(TOPK):
                            pool.indirect_dma_start(
                                out=rows[:, s % SLOTS, k, :], out_offset=None, in_=table[:, :],
                                in_offset=bass.IndirectOffsetOnAxis(ap=row[:, t, h, k:k + 1], axis=0),
                            ).then_inc(fetched[s % SLOTS], 16)
                    for i in range(SLOTS):
                        pool.wait_ge(fetched[i], 16 * TOPK * (STEPS // SLOTS))
                    pool.dma_reset(range(fetched[0].num, fetched[-1].num + 1))

                @block.scalar
                def _(act):
                    chain = [0]

                    def norm(k):
                        act.wait_ge(xT_psum, k + 1)
                        nc.scalar.copy(xT[:, :], f0[:, 0:TOKENS]).then_inc(xT_up, 1)

                    def gat_a(n):
                        act.wait_ge(gat_psum, n + 1)
                        src = f2[:, :].rearrange("p (t c) -> p t c", t=TILES)[:, :, 0:D + 1]
                        nc.scalar.copy(gat_h[:, :, :], src).then_inc(gat_h_up, 1)
                        act.wait_ge(gat_h_up, n + 1)
                        for t in range(TILES):
                            ins = nc.scalar.activation(edge[:, t, :], f1[:, 0:TOKENS], ACT.Identity,
                                                       bias=gat_h[:, t, D:D + 1])
                        ins.then_inc(edge_up, 1)

                    def gat_b(n):
                        act.wait_ge(nmax_up, n + 1)
                        for t in range(TILES):
                            ins = nc.scalar.activation(edge[:, t, :], edge_m[:, t, :], ACT.Exp,
                                                       bias=edge_nmax[:, t:t + 1], accum_out=edge_sum[:, t:t + 1])
                        ins.then_inc(edge_exp, 1)
                        act.wait_ge(edge_T_psum, n + 1)
                        nc.scalar.copy(edge_T[:, :], f1[:, :]).then_inc(edge_T_up, 1)

                    def gat_c(n):
                        act.wait_ge(elu_in, n + 1)
                        nc.scalar.activation(elu_exp[:, :, :], elu_neg[:, :, :], ACT.Exp).then_inc(elu_up, 1)

                    def gate():
                        act.wait_ge(gap_up, 1)
                        nc.scalar.activation(gap_exp[:, :], gap[:, :], ACT.Exp).then_inc(gap_exp_up, 1)

                    def moe(q):
                        for e in range(4 * q, 4 * q + 4):
                            act.wait_ge(h1_psum, e + 1)
                            if e >= 2:
                                act.wait_ge(hid_up, e - 1)
                            nc.scalar.activation(tanh_h[:, e % 2, :], (f0, f2)[e % 2][:, :], ACT.Tanh,
                                                 scale=0.5).then_inc(tanh_up, 1)

                    def keys(n):
                        if n % 2:
                            act.wait_ge(fin_up, n // 2 + 1)
                            nc.scalar.activation(fin_e[:, :, :], fin_s[:, :, :], ACT.Exp).then_inc(fin_exp, 1)

                    def attend_a(n):
                        act.wait_ge(qk_psum, n + 1)
                        nc.scalar.mul(qk_sb[:, 0:TOKENS], p_qk[:, 0:TOKENS], float(D) ** -0.5)
                        nc.scalar.copy(qk_sb[:, TOKENS:], p_qk[:, TOKENS:]).then_inc(qk_up, 1)

                    def attend_b(n):
                        act.wait_ge(sim_nmax_up, n + 1)
                        nc.scalar.activation(prob[:, 0:P], sim[:, 0:P], ACT.Exp, bias=sim_nmax[:, 0:1],
                                             accum_out=sim_sum[:, 0:1])
                        nc.scalar.activation(prob[:, P:], sim[:, P:], ACT.Exp, bias=sim_nmax[:, 1:2],
                                             accum_out=sim_sum[:, 1:2]).then_inc(sim_exp, 1)

                    def attend_c(h, n):
                        act.wait_ge(prob_T_psum, n + 1)
                        nc.scalar.copy(prob_T[:, :], p_tr[:, 0:3 * P]).then_inc(prob_T_up, 1)
                        act.wait_ge(att_psum, n + 1)
                        nc.scalar.copy(att_T[:, h, :], p_qk[:, 0:TOKENS]).then_inc(att_up, 1)

                    def front_part(name):
                        run = {"norm": norm, "gat_a": gat_a, "gat_b": gat_b, "gat_c": gat_c, "moe": moe,
                               "keys": keys}
                        if name == "gate":
                            gate()
                        else:
                            run[name[:-1]](int(name[-1]))

                    if tail:
                        attend_a(0)
                        attend_b(0)
                        attend_c(HEADS - 1, 0)
                    for s in range(STEPS):
                        h = s // TILES - 1
                        if gather and h >= 0 and s % TILES == 0:
                            attend_a(nth[h])
                        if gather and h >= 0 and s % TILES == 1:
                            attend_c(h, nth[h])
                        if gather and h >= 0 and s % TILES == 0:
                            attend_b(nth[h])
                        if front:
                            for name in front_parts(s):
                                front_part(name)

                @block.tensor
                def _(pe):
                    def norm(k):
                        pe.wait_ge(normed_up, k + 1)
                        for t in range(TILES):
                            mm = nc.tensor.transpose(f0[:, t * P:(t + 1) * P], normed[:, t, :], ident)
                        mm.then_inc(xT_psum, 1)

                    def gat_a(n):
                        pe.wait_ge(xT_up, 2 * n + 1)
                        nc.tensor.matmul(f1[:, 0:TOKENS], gat_dst[:, n, :], xT[:, :], start=True, stop=True)
                        for t in range(TILES):
                            mm = nc.tensor.matmul(f2[:, t * 256:t * 256 + D + 1], xT[:, t * P:(t + 1) * P],
                                                  gat_ext[:, n, :], start=True, stop=True)
                        mm.then_inc(gat_psum, 1)

                    def gat_b(n):
                        pe.wait_ge(edge_exp, n + 1)
                        for t in range(TILES):
                            for j in range(TILES):
                                mm = nc.tensor.transpose(f1[:, j * TOKENS + t * P:j * TOKENS + (t + 1) * P],
                                                         edge[:, t, j * P:(j + 1) * P], ident)
                        mm.then_inc(edge_T_psum, 1)
                        pe.wait_ge(edge_T_up, n + 1)
                        for t in range(TILES):
                            for j in range(TILES):
                                mm = nc.tensor.matmul(f0[:, t * P:(t + 1) * P],
                                                      edge_T[:, j * TOKENS + t * P:j * TOKENS + (t + 1) * P],
                                                      gat_h[:, j, 0:D], start=(j == 0), stop=(j == TILES - 1))
                        mm.then_inc(gat_out, 1)

                    def gat_c(n):
                        pass

                    def gate():
                        pe.wait_ge(xT_up, 2)
                        for t in range(TILES):
                            mm = nc.tensor.matmul(f1[:, t * EXPERTS:(t + 1) * EXPERTS], xT[:, t * P:(t + 1) * P],
                                                  gate_w_sb[:, :], start=True, stop=True)
                        mm.then_inc(logits_psum, 1)

                    def moe_up(e):
                        if e == 1:
                            pe.wait_ge(gap_up, 1)
                        if e >= 2:
                            pe.wait_ge(hid_up, e - 1)
                        for w, bank, signal in ((w1_sb, (f0, f2)[e % 2], h1_psum), (w2_sb, (f1, f3)[e % 2], h2_psum)):
                            if e == 0 and w is w2_sb:
                                pe.wait_ge(gap_up, 1)
                            for c in range(CHUNKS):
                                mm = nc.tensor.matmul(bank[:, c * TOKENS:(c + 1) * TOKENS],
                                                      w[:, e, c * P:(c + 1) * P], xT[:, :], start=True, stop=True)
                            mm.then_inc(signal, 1)

                    def moe_down(e):
                        pe.wait_ge(hid_up, e + 1)
                        if e:
                            pe.wait_ge(moe_added, e)
                        for t in range(TILES):
                            for c in range(CHUNKS):
                                mm = nc.tensor.matmul(f4[:, t * P:(t + 1) * P],
                                                      hid[:, e % 2, c, t * P:(t + 1) * P],
                                                      w3_sb[:, CHUNKS * e + c, :], start=(c == 0),
                                                      stop=(c == CHUNKS - 1))
                        mm.then_inc(moe_psum, 1)

                    def moe(q):
                        for e in range(4 * q, 4 * q + 4):
                            moe_up(e)
                            if e:
                                moe_down(e - 1)
                        if q == 3:
                            moe_down(EXPERTS - 1)

                    def keys(n):
                        t = n // 2
                        pe.wait_ge(xT_up, 4)
                        for u in range(2):
                            c = 2 * (n % 2) + u
                            g = 2 * n + u
                            if g >= 2:
                                pe.wait_ge(scores_read, g - 1)
                            nc.tensor.matmul((f2, f3)[g % 2][:, :], xT[:, t * P:(t + 1) * P],
                                             pk_mat[:, c * 512:(c + 1) * 512], start=True,
                                             stop=True).then_inc(scores_psum, 1)

                    def attend_a(h, n):
                        if n >= 1:
                            pe.wait_ge(att_up, n)
                        nc.tensor.matmul(p_qk[:, 0:TOKENS], wq_sb[:, h * D:(h + 1) * D], xT_cur[:, :],
                                         start=True, stop=True)
                        for t in range(TILES):
                            mm = nc.tensor.transpose(p_qk[:, TOKENS + t * P:TOKENS + (t + 1) * P],
                                                     kv[:, h % 2, t, 0:D], ident)
                        mm.then_inc(qk_psum, 1)
                        pe.wait_ge(qk_up, n + 1)
                        nc.tensor.matmul(p_sim[:, 0:P], qk_sb[:, 0:P], qk_sb[:, TOKENS:TOKENS + P], start=True,
                                         stop=True)
                        nc.tensor.matmul(p_sim[:, P:3 * P], qk_sb[:, P:2 * P], qk_sb[:, TOKENS:], start=True,
                                         stop=True).then_inc(sim_psum, 1)

                    def attend_c(h, n):
                        pe.wait_ge(prob_up, n + 1)
                        for c in range(3):
                            mm = nc.tensor.transpose(p_tr[:, c * P:(c + 1) * P], prob[:, c * P:(c + 1) * P], ident)
                        mm.then_inc(prob_T_psum, 1)
                        pe.wait_ge(prob_T_up, n + 1)
                        nc.tensor.matmul(p_qk[:, 0:TOKENS], kv[:, h % 2, 0, D:], prob_T[:, 0:TOKENS], start=True,
                                         stop=False)
                        nc.tensor.matmul(p_qk[:, P:TOKENS], kv[:, h % 2, 1, D:], prob_T[:, TOKENS:], start=False,
                                         stop=True).then_inc(att_psum, 1)

                    def front_part(name):
                        run = {"norm": norm, "gat_a": gat_a, "gat_b": gat_b, "gat_c": gat_c, "moe": moe,
                               "keys": keys}
                        if name == "gate":
                            gate()
                        else:
                            run[name[:-1]](int(name[-1]))

                    if tail:
                        pe.wait_ge(slot_free, 1)
                        attend_a(HEADS - 1, 0)
                        attend_c(HEADS - 1, 0)
                        pe.wait_ge(att_up, 1)
                        for t in range(TILES):
                            for h in range(HEADS):
                                mm = nc.tensor.matmul(p_sim[:, t * P:(t + 1) * P], att_T[:, h, t * P:(t + 1) * P],
                                                      wo_sb[:, h, :], start=(h == 0), stop=(h == HEADS - 1))
                        mm.then_inc(y_psum, 1)
                    for s in range(STEPS):
                        h = s // TILES - 1
                        if gather and h >= 0 and s % TILES == 0:
                            if h == 0:
                                pe.wait_ge(handed, 1)
                            pe.wait_ge(slot_free, TILES * (h + 1) + (1 if tail else 0))
                            attend_a(h, nth[h])
                        if gather and h >= 0 and s % TILES == 1:
                            attend_c(h, nth[h])
                        if front:
                            for name in front_parts(s):
                                front_part(name)

                @block.vector
                def _(dve):
                    chain = [0]

                    def link(ins):
                        chain[0] += 1
                        ins.then_inc(dve_step, 1)
                        dve.wait_ge(dve_step, chain[0])

                    def step(ins):
                        chain[0] += 1
                        ins.then_inc(dve_step, 1)
                        return chain[0]

                    v = nc.vector

                    def norm(k):
                        if k == 0:
                            dve.wait_ge(x_loaded, 16)
                        for t in range(TILES):
                            last = step(v.bn_stats(stats[:, t, :], res[:, t, :]))
                        dve.wait_ge(dve_step, last)
                        for t in range(TILES):
                            last = step(v.bn_aggr(meanvar[:, t, :], stats[:, t, :]))
                        dve.wait_ge(dve_step, last)
                        link(v.tensor_scalar(var_eps[:, :], meanvar[:, :, 1], EPS, None, ALU.add))
                        link(v.tensor_scalar(rs_i[:, :], var_eps[:, :].bitcast(I32), 1, None,
                                             ALU.logical_shift_right))
                        link(v.tensor_scalar(rs_y[:, :].bitcast(I32), rs_i[:, :], -1.0, float(RSQRT_MAGIC), ALU.mult,
                                             ALU.add))
                        for _ in range(3):
                            link(v.tensor_tensor(rs_t[:, :], rs_y[:, :], rs_y[:, :], ALU.mult))
                            link(v.scalar_tensor_tensor(out=rs_t[:, :], in0=rs_t[:, :], scalar=-0.5,
                                                        in1=var_eps[:, :], op0=ALU.mult, op1=ALU.mult))
                            link(v.scalar_tensor_tensor(out=rs_y[:, :], in0=rs_t[:, :], scalar=1.5, in1=rs_y[:, :],
                                                        op0=ALU.add, op1=ALU.mult))
                        for t in range(TILES):
                            ins = v.tensor_scalar(normed[:, t, :], res[:, t, :], meanvar[:, t, 0:1],
                                                  rs_y[:, t:t + 1], ALU.subtract, ALU.mult)
                        ins.then_inc(normed_up, 1)

                    def gat_a(n):
                        dve.wait_ge(edge_up, n + 1)
                        for t in range(TILES):
                            last = step(v.scalar_tensor_tensor(out=edge_l[:, t, :], in0=edge[:, t, :], scalar=SLOPE,
                                                               in1=edge[:, t, :], op0=ALU.mult, op1=ALU.max))
                        dve.wait_ge(dve_step, last)
                        for t in range(TILES):
                            last = step(v.tensor_tensor_reduce(edge_m[:, t, :], edge_l[:, t, :], adj_bias[:, t, :], 1.0,
                                                               LOWEST, ALU.add, ALU.max, edge_max[:, t:t + 1]))
                        dve.wait_ge(dve_step, last)
                        v.tensor_scalar(edge_nmax[:, :], edge_max[:, :], -1.0, None, ALU.mult).then_inc(nmax_up, 1)

                    def gat_b(n):
                        dve.wait_ge(edge_exp, n + 1)
                        link(v.reciprocal(edge_inv[:, :], edge_sum[:, :]))

                    def gat_c(n):
                        dve.wait_ge(gat_out, n + 1)
                        for t in range(TILES):
                            ins = v.tensor_scalar(elu_neg[:, t, :], f0[:, t * P:(t + 1) * P], edge_inv[:, t:t + 1],
                                                  0.0, ALU.mult, ALU.min)
                        ins.then_inc(elu_in, 1)
                        for t in range(TILES):
                            last = step(v.tensor_scalar(elu_pos[:, t, :], f0[:, t * P:(t + 1) * P],
                                                        edge_inv[:, t:t + 1], 0.0, ALU.mult, ALU.max))
                        dve.wait_ge(dve_step, last)
                        dve.wait_ge(elu_up, n + 1)
                        link(v.scalar_tensor_tensor(out=elu_pos[:, :, :], in0=elu_exp[:, :, :], scalar=-1.0,
                                                    in1=elu_pos[:, :, :], op0=ALU.add, op1=ALU.add))
                        link(v.tensor_tensor(res[:, :, :], res[:, :, :], elu_pos[:, :, :], ALU.add))

                    def gate():
                        dve.wait_ge(logits_psum, 1)
                        for t in range(TILES):
                            last = step(v.tensor_tensor(logits[:, t, :], f1[:, t * EXPERTS:(t + 1) * EXPERTS],
                                                        gate_b_sb[:, :], ALU.add))
                        dve.wait_ge(dve_step, last)
                        for t in range(TILES):
                            last = step(v.max(best[:, t, :], logits[:, t, :]))
                        dve.wait_ge(dve_step, last)
                        v.tensor_tensor(gap[:, :], best[:, :, 1], best[:, :, 0], ALU.subtract).then_inc(gap_up, 1)
                        for t in range(TILES):
                            last = step(v.max_index(best_i[:, t, :], best[:, t, :], logits[:, t, :]))
                        dve.wait_ge(dve_step, last)
                        link(v.tensor_copy(best_f[:, :, :], best_i[:, :, 0:2]))
                        dve.wait_ge(gap_exp_up, 1)
                        link(v.tensor_scalar(gate_den[:, :], gap_exp[:, :], 1.0, None, ALU.add))
                        link(v.reciprocal(gate_p[:, :, 0], gate_den[:, :]))
                        link(v.tensor_tensor(gate_p[:, :, 1], gate_p[:, :, 0], gap_exp[:, :], ALU.mult))
                        for t in range(TILES):
                            for k in range(2):
                                last = step(v.tensor_scalar(disp[:, t, k, :], iota[:, 0:EXPERTS],
                                                            best_f[:, t, k:k + 1], gate_p[:, t, k:k + 1],
                                                            ALU.is_equal, ALU.mult))
                        dve.wait_ge(dve_step, last)
                        link(v.tensor_tensor(dispatch[:, :, :], disp[:, :, 0, :], disp[:, :, 1, :], ALU.add))

                    def moe_hid(e):
                        dve.wait_ge(tanh_up, e + 1)
                        if e >= 2:
                            dve.wait_ge(hid_up, e - 1)
                        link(v.scalar_tensor_tensor(out=silu_h[:, e % 2, :], in0=tanh_h[:, e % 2, :], scalar=1.0,
                                                    in1=(f0, f2)[e % 2][:, :], op0=ALU.add, op1=ALU.mult))
                        dve.wait_ge(h2_psum, e + 1)
                        if e >= 2:
                            dve.wait_ge(moe_psum, e - 1)
                        v.scalar_tensor_tensor(out=hid[:, e % 2, :, :].rearrange("p c n -> p (c n)"),
                                               in0=silu_h[:, e % 2, :], scalar=0.5, in1=(f1, f3)[e % 2][:, :],
                                               op0=ALU.mult, op1=ALU.mult).then_inc(hid_up, 1)

                    def moe_add(e):
                        dve.wait_ge(moe_psum, e + 1)
                        if e:
                            dve.wait_ge(moe_added, e)
                        for t in range(TILES):
                            ins = v.scalar_tensor_tensor(out=res[:, t, :],
                                                         in0=f4[:, t * P:(t + 1) * P],
                                                         scalar=dispatch[:, t, e:e + 1], in1=res[:, t, :],
                                                         op0=ALU.mult, op1=ALU.add)
                        ins.then_inc(moe_added, 1)

                    def moe(q):
                        for e in range(4 * q, 4 * q + 4):
                            moe_hid(e)
                            if e:
                                moe_add(e - 1)
                        if q == 3:
                            moe_add(EXPERTS - 1)
                            dve.wait_ge(moe_added, EXPERTS)

                    def top16(best_out, index_out, rest_of, scores):
                        n = range(len(scores))
                        for i in n:
                            last = step(v.max(best_out[i][:, 0:8], scores[i]))
                        dve.wait_ge(dve_step, last)
                        for i in n:
                            last = step(v.match_replace(rest_of[i], best_out[i][:, 0:8], scores[i], LOWEST))
                        for i in n:
                            step(v.max_index(index_out[i][:, 0:8], best_out[i][:, 0:8], scores[i]))
                        dve.wait_ge(dve_step, last)
                        for i in n:
                            last = step(v.max(best_out[i][:, 8:16], rest_of[i]))
                        dve.wait_ge(dve_step, last)
                        for i in n:
                            last = step(v.max_index(index_out[i][:, 8:16], best_out[i][:, 8:16], rest_of[i]))
                        return last

                    def keys(n):
                        t = n // 2
                        for u in range(2):
                            g = 2 * n + u
                            bank = (f2, f3)[g % 2]
                            dve.wait_ge(scores_psum, g + 1)
                            for i in range(2):
                                h = (2 * (n % 2) + u) * 2 + i
                                last = top16([sc[:, h, p, :] for p in range(2)], [ix[:, h, p, :] for p in range(2)],
                                             [rest[:, p, :] for p in range(2)],
                                             [bank[:, (2 * i + p) * KEYS:(2 * i + p + 1) * KEYS] for p in range(2)])
                                dve.wait_ge(dve_step, last)
                            v.engine_nop().then_inc(scores_read, 1)
                        if n % 2:
                            pairs(t)

                    def pairs(t):
                        link(v.tensor_copy(ixf[:, :, :, :], ix[:, :, :, :]))
                        link(v.tensor_scalar(ixf[:, :, 1, :], ixf[:, :, 1, :], float(KEYS), None, ALU.mult))
                        for src, dst in ((sc, pair_s), (ixf, pair_i)):
                            for i in range(SINGLES):
                                w = PAIR_ROWS[i]
                                last = step(v.tensor_tensor(dst[:, :, PAIR_AT[i]:PAIR_AT[i] + w],
                                                            src[:, :, 1, 0:w],
                                                            src[:, :, 0, i:i + 1].to_broadcast([P, HEADS, w]),
                                                            ALU.add))
                            last = step(v.tensor_tensor(dst[:, :, PAIR_AT[SINGLES]:], src[:, :, 0, SINGLES:],
                                                        src[:, :, 1, 0:1].to_broadcast([P, HEADS, TOPK - SINGLES]),
                                                        ALU.add))
                        dve.wait_ge(dve_step, last)
                        for h in range(0, HEADS, 2):
                            last = top16([fin_s[:, h + i, :] for i in range(2)], [fin_p[:, h + i, :] for i in range(2)],
                                         [rest2[:, i, :] for i in range(2)], [pair_s[:, h + i, :] for i in range(2)])
                            dve.wait_ge(dve_step, last)
                        link(v.tensor_copy(fin_pf[:, :, :], fin_p[:, :, :]))
                        link(v.tensor_scalar(fin_sum[:, :], fin_s[:, :, 0], 1.0, None, ALU.mult))
                        v.tensor_tensor(fin_s[:, :, :], fin_s[:, :, :],
                                        fin_sum[:, :].unsqueeze(2).to_broadcast([P, HEADS, TOPK]),
                                        ALU.subtract).then_inc(fin_up, 1)
                        for h in range(0, HEADS, 2):
                            for i in range(2):
                                last = step(v.tensor_tensor(
                                    hit[:, i, :, :], iota.unsqueeze(1).to_broadcast([P, TOPK, PAIRS]),
                                    fin_pf[:, h + i, :].unsqueeze(2).to_broadcast([P, TOPK, PAIRS]), ALU.is_equal))
                            dve.wait_ge(dve_step, last)
                            for i in range(2):
                                last = step(v.tensor_tensor(
                                    hit[:, i, :, :], hit[:, i, :, :],
                                    pair_i[:, h + i, :].unsqueeze(1).to_broadcast([P, TOPK, PAIRS]), ALU.mult))
                            dve.wait_ge(dve_step, last)
                            for i in range(2):
                                last = step(v.tensor_reduce(fin_i[:, h + i, :], hit[:, i, :, :], AX.X, ALU.add))
                            dve.wait_ge(dve_step, last)
                        step(v.tensor_tensor(row_next[:, t, :, :], fin_i[:, :, :],
                                             head_row.rearrange("p (h k) -> p h k", h=HEADS), ALU.add))
                        dve.wait_ge(fin_exp, t + 1)
                        link(v.tensor_reduce(fin_sum[:, :], fin_e[:, :, :], AX.X, ALU.add))
                        link(v.reciprocal(fin_sum[:, :], fin_sum[:, :]))
                        link(v.tensor_tensor(wt_next[:, t, :, :], fin_e[:, :, :],
                                             fin_sum[:, :].unsqueeze(2).to_broadcast([P, HEADS, TOPK]), ALU.mult))

                    def combine(s, in_tail=False):
                        h, t = s // TILES, s % TILES
                        if not in_tail:
                            dve.wait_ge(fetched[s % SLOTS], 16 * TOPK * (s // SLOTS + 1))
                        before = h - 2 if h >= 2 else HEADS - 1
                        if not in_tail and (h >= 2 or (h == 1 and tail)):
                            dve.wait_ge(att_psum, nth[before] + 1)
                        summed = 0 if in_tail else s + (1 if tail else 0)
                        if summed:
                            dve.wait_ge(slot_free, summed)
                        sums = (kv[:, h % 2, t, :], part[:, :])
                        lasts = [0, 0]
                        for k in range(TOPK):
                            src, w, to = rows[:, s % SLOTS, k, :], wt[:, t, h, k:k + 1], sums[k % 2]
                            if k < 2:
                                lasts[k] = step(v.tensor_scalar(to, src, w, None, ALU.mult))
                            else:
                                dve.wait_ge(dve_step, lasts[k % 2])
                                lasts[k % 2] = step(v.scalar_tensor_tensor(out=to, in0=src, scalar=w, in1=to,
                                                                           op0=ALU.mult, op1=ALU.add))
                        dve.wait_ge(dve_step, lasts[1])
                        v.tensor_tensor(sums[0], sums[0], sums[1], ALU.add).then_inc(slot_free, 1)

                    def attend_max(n):
                        dve.wait_ge(sim_psum, n + 1)
                        step(v.tensor_tensor_reduce(sim[:, 0:P], p_sim[:, 0:P], causal[:, P:], 1.0, LOWEST, ALU.add,
                                                    ALU.max, sim_max[:, 0:1]))
                        link(v.tensor_tensor_reduce(sim[:, P:], p_sim[:, P:3 * P], causal, 1.0, LOWEST, ALU.add,
                                                    ALU.max, sim_max[:, 1:2]))
                        v.tensor_scalar(sim_nmax[:, :], sim_max[:, :], -1.0, None, ALU.mult).then_inc(sim_nmax_up, 1)

                    def attend_norm(n):
                        dve.wait_ge(sim_exp, n + 1)
                        link(v.reciprocal(sim_inv[:, :], sim_sum[:, :]))
                        v.tensor_scalar(prob[:, 0:P], prob[:, 0:P], sim_inv[:, 0:1], None, ALU.mult)
                        v.tensor_scalar(prob[:, P:], prob[:, P:], sim_inv[:, 1:2], None, ALU.mult).then_inc(prob_up, 1)

                    def front_part(name):
                        run = {"norm": norm, "gat_a": gat_a, "gat_b": gat_b, "gat_c": gat_c, "moe": moe,
                               "keys": keys}
                        if name == "gate":
                            gate()
                        else:
                            run[name[:-1]](int(name[-1]))

                    if gather:
                        v.tensor_copy(row[:, :, :, :], row_next[:, :, :, :]).then_inc(handed_rows, 1)
                    if tail:
                        combine(STEPS - 1, in_tail=True)
                        attend_max(0)
                        attend_norm(0)
                        dve.wait_ge(y_psum, 1)
                        v.tensor_tensor(y_sb[:, :, :], p_sim[:, 0:TOKENS].rearrange("p (t d) -> p t d", t=TILES),
                                        res_cur[:, :, :], ALU.add).then_inc(y_up, 1)
                        dve.wait_ge(y_up, 1)
                    if gather:
                        v.tensor_copy(wt[:, :, :, :], wt_next[:, :, :, :])
                        v.tensor_copy(xT_cur[:, :], xT[:, :])
                        v.tensor_copy(res_cur[:, :, :], res[:, :, :]).then_inc(handed, 1)
                        dve.wait_ge(handed, 1)
                    for s in range(STEPS):
                        h = s // TILES - 1
                        if gather and h >= 0 and s % TILES == 1:
                            attend_norm(nth[h])
                        if gather and s < STEPS - 1:
                            combine(s)
                        if gather and h >= 0 and s % TILES == 0:
                            attend_max(nth[h])
                        if front:
                            for name in front_parts(s):
                                front_part(name)
            clear_semaphores()

        run_pass(0, front=True, gather=False, tail=False)
        run_pass(0, front=True, gather=True, tail=False)
        with nc.Fori(1, BATCHES - 1) as b:
            run_pass(b, front=True, gather=True, tail=True)
        run_pass(BATCHES - 1, front=False, gather=True, tail=True)
        run_pass(BATCHES, front=False, gather=False, tail=True)


def kernel(**inputs):
    import concourse.bacc as _bacc
    from concourse.bass_utils import run_bass_kernel_spmd as _run

    a = {k: np.asarray(v) for k, v in inputs.items()}
    nc = _bacc.Bacc("TRN2", target_bir_lowering=False, num_devices=1)
    arrays = {
        "x": a["x"],
        "adj": a["adj"],
        "consts": shape_constants(),
        "gat_w": np.stack([a["L0_gnn_W"], a["L1_gnn_W"]], axis=1),
        "gat_wt": np.stack([a["L0_gnn_W"].T, a["L1_gnn_W"].T], axis=1),
        "gat_a": np.stack([a["L0_gnn_a"].reshape(2, D).T, a["L1_gnn_a"].reshape(2, D).T], axis=1),
        "gate_w": a["L0_ffn_gate_w"],
        "gate_b": np.broadcast_to(a["L0_ffn_gate_b"][None, :], (P, EXPERTS)),
        "w1": a["L0_ffn_w1"],
        "w2": a["L0_ffn_w2"],
        "w3": a["L0_ffn_w3"],
        "pk_wt": a["L1_ffn_Wq_pk"].reshape(D, 2, HEADS, DK).transpose(3, 2, 1, 0).reshape(DK, 2 * HEADS * D),
        "pk_kt": a["L1_ffn_pk_keys"].transpose(3, 2, 0, 1).reshape(DK, 2 * HEADS * KEYS),
        "wq": a["L1_ffn_Wq"],
        "table": np.concatenate([a["L1_ffn_keys_table"], a["L1_ffn_values_table"]], axis=1),
        "wo": a["L1_ffn_Wo"],
    }
    arrays = {f"in_{k}_dram": np.ascontiguousarray(v) for k, v in arrays.items()}
    args = [nc.dram_tensor(k, v.shape, mybir.dt.from_np(v.dtype), kind="ExternalInput").ap()
            for k, v in arrays.items()]
    args.append(nc.dram_tensor("out_0_dram", a["x"].shape, F32, kind="ExternalOutput").ap())
    build(nc, *args)
    r = _run(nc, [arrays], core_ids=[0])
    return r.results[0]["out_0_dram"]
```

```python
from contextlib import ExitStack

import numpy as np

import concourse.bass as bass
from concourse import mybir

F32 = mybir.dt.float32
U32 = mybir.dt.uint32
I32 = mybir.dt.int32
ALU = mybir.AluOpType
ACT = mybir.ActivationFunctionType
AX = mybir.AxisListType

P = 128
D = 128
TOKENS = 256
TILES = TOKENS // P
EXPERTS = 16
HIDDEN = 256
CHUNKS = HIDDEN // P
HEADS = 8
KEYS = 128
DK = D // 2
TOPK = 16
STEPS = HEADS * TILES
SLOTS = 4
FETCH_SEMS = 8
EARLY = [0, 2]
LATE = TILES
EPS = 1e-5
SLOPE = 0.2
NEG_BIG = -9e15
LOWEST = -3.0e38
RSQRT_MAGIC = 0x5F3759DF

PAIR_ROWS = [TOPK // (i + 1) for i in range(TOPK)]
PAIR_AT = [sum(PAIR_ROWS[:i]) for i in range(TOPK)]
PAIRS = sum(PAIR_ROWS)
SINGLES = PAIR_ROWS.index(1)

C_IDENT = 0
C_CAUSAL = C_IDENT + P
C_IOTA = C_CAUSAL + 2 * P
C_HEAD = C_IOTA + PAIRS
C_PAIR = C_HEAD + HEADS * TOPK
C_ALL = C_PAIR + PAIRS


def shape_constants():
    c = np.zeros((P, C_ALL), np.float32)
    c[:, C_IDENT:C_IDENT + P] = np.eye(P)
    i = np.arange(P)
    c[:, C_CAUSAL + P:C_CAUSAL + 2 * P] = np.where(i[None, :] <= i[:, None], 0.0, LOWEST)
    c[:, C_IOTA:C_IOTA + PAIRS] = np.arange(PAIRS)
    c[:, C_HEAD:C_HEAD + HEADS * TOPK] = np.repeat(np.arange(HEADS) * KEYS * KEYS, TOPK)
    c[:, C_PAIR:C_PAIR + PAIRS] = np.arange(PAIRS) * KEYS * KEYS
    return c


def build(nc, x, adj, consts, gat_w, gat_wt, gat_a, gate_w, gate_b, w1, w2, w3, pk_wt, pk_kt, wq, table, wo, out):
    BATCHES = x.shape[0]

    with ExitStack() as ctx:
        def sb(name, shape, dt=F32):
            return ctx.enter_context(nc.sbuf_tensor(name, shape, dt))

        def ps(name):
            return ctx.enter_context(nc.psum_tensor(name, [P, 512], F32))

        sems = []

        def sem(name):
            s = ctx.enter_context(nc.semaphore(name))
            sems.append(s)
            return s

        const = sb("const", [P, C_ALL])
        ident = const[:, C_IDENT:C_IDENT + P]
        causal = const[:, C_CAUSAL:C_CAUSAL + 2 * P]
        iota = const[:, C_IOTA:C_IOTA + PAIRS]
        pair_code = const[:, C_PAIR:C_PAIR + PAIRS]
        head_row = const[:, C_HEAD:C_HEAD + HEADS * TOPK]
        w1_sb = sb("w1_sb", [P, EXPERTS, HIDDEN])
        w2_sb = sb("w2_sb", [P, EXPERTS, HIDDEN])
        w3_sb = sb("w3_sb", [P, EXPERTS * CHUNKS, D])
        gate_w_sb = sb("gate_w_sb", [P, EXPERTS])
        gate_b_sb = sb("gate_b_sb", [P, EXPERTS])
        wq_sb = sb("wq_sb", [P, HEADS * D])
        wo_sb = sb("wo_sb", [P, HEADS, D])
        gat_ext = sb("gat_ext", [P, 2, D + 1])
        gat_dst = sb("gat_dst", [P, 2, P])
        adj_bias = sb("adj_bias", [P, TILES, TOKENS])
        pk_mat = sb("pk_mat", [P, HEADS * 2 * KEYS])

        res_a = sb("res_a", [P, TILES, D])
        res_b = sb("res_b", [P, TILES, D])
        xT_a = sb("xT_a", [P, TOKENS])
        xT_b = sb("xT_b", [P, TOKENS])
        act_h = sb("act_h", [P, CHUNKS * TOKENS])
        hid = sb("hid", [P, 2, CHUNKS, TOKENS])
        stats = sb("stats", [P, TILES, 6])
        meanvar = sb("meanvar", [P, TILES, 2])
        rs_i = sb("rs_i", [P, TILES], I32)
        rs_y = sb("rs_y", [P, TILES])
        rs_t = sb("rs_t", [P, TILES])
        var_eps = sb("var_eps", [P, TILES])
        normed = sb("normed", [P, TILES, D])
        gat_h = sb("gat_h", [P, TILES, D + 1])
        edge = hid[:, 0, :, :]
        edge_max = sb("edge_max", [P, TILES])
        edge_nmax = sb("edge_nmax", [P, TILES])
        edge_sum = sb("edge_sum", [P, TILES])
        edge_inv = sb("edge_inv", [P, TILES])
        edge_T = act_h
        elu_neg = edge[:, :, 0:D]
        elu_exp = edge[:, :, D:]
        elu_pos = normed
        logits = sb("logits", [P, TILES, EXPERTS])
        best = sb("best", [P, TILES, 8])
        best_i = sb("best_i", [P, TILES, 8], U32)
        best_f = sb("best_f", [P, TILES, 2])
        gap = sb("gap", [P, TILES])
        gap_exp = sb("gap_exp", [P, TILES])
        gate_den = sb("gate_den", [P, TILES])
        gate_p = sb("gate_p", [P, TILES, 2])
        disp = sb("disp", [P, TILES, 2, EXPERTS])
        dispatch = sb("dispatch", [P, TILES, EXPERTS])
        chosen = sb("chosen", [P, 4, PAIRS])
        code = sb("code", [P, HEADS, TOPK])
        code_i = sb("code_i", [P, HEADS, TOPK], I32)
        code_p = sb("code_p", [P, HEADS, TOPK])
        hit = sb("hit", [P, 4, TOPK, TOPK])
        rest = sb("rest", [P, 2, KEYS])
        sc = sb("sc", [P, HEADS, 2, TOPK])
        ix = sb("ix", [P, HEADS, 2, TOPK], U32)
        ixf = sb("ixf", [P, HEADS, 2, TOPK])
        pair_s = sb("pair_s", [P, HEADS, PAIRS])
        pair_i = sb("pair_i", [P, HEADS, PAIRS])
        rest2 = sb("rest2", [P, 4, PAIRS])
        fin_s = sb("fin_s", [P, HEADS, TOPK])
        fin_p = sb("fin_p", [P, HEADS, TOPK], U32)
        fin_pf = sb("fin_pf", [P, HEADS, TOPK])
        fin_i = sb("fin_i", [P, HEADS, TOPK])
        fin_e = sb("fin_e", [P, HEADS, TOPK])
        fin_sum = sb("fin_sum", [P, HEADS])
        row_next = sb("row_next", [P, TILES, HEADS, TOPK], U32)
        wt_next = sb("wt_next", [P, TILES, HEADS, TOPK])

        row = sb("row", [P, TILES, HEADS, TOPK], U32)
        wt = sb("wt", [P, TILES, HEADS, TOPK])
        xT_cur = sb("xT_cur", [P, TOKENS])
        res_cur = sb("res_cur", [P, TILES, D])
        xT_prev = sb("xT_prev", [P, TOKENS])
        res_prev = sb("res_prev", [P, TILES, D])
        rows = sb("rows", [P, SLOTS, TOPK, 2 * D])
        diag = sb("diag", [P, 2, TOPK, P])
        kv = sb("kv", [P, 2, TILES, 2 * D])
        qk_sb = sb("qk_sb", [P, 2 * TOKENS])
        sim = sb("sim", [P, 3 * P])
        sim_max = sb("sim_max", [P, TILES])
        sim_nmax = sb("sim_nmax", [P, TILES])
        sim_sum = sb("sim_sum", [P, TILES])
        sim_inv = sb("sim_inv", [P, TILES])
        prob = sb("prob", [P, 3 * P])
        prob_T = sb("prob_T", [P, 3 * P])
        att_T = sb("att_T", [P, HEADS, TOKENS])
        y_sb = res_prev

        a0, a1, a2, b0, b1 = (ps(name) for name in ("a0", "a1", "a2", "b0", "b1"))
        p_qk, p_sim, p_sum = ps("p_qk"), ps("p_sim"), ps("p_sum")

        fetched = [ctx.enter_context(nc.semaphore(f"fetched{i}")) for i in range(FETCH_SEMS)]
        weights_loaded = ctx.enter_context(nc.semaphore("weights_loaded"))
        loaded = sem("loaded")
        ext_psum = sem("ext_psum")
        setup_mat = sem("setup_mat")
        setup_mat_sb = sem("setup_mat_sb")
        dve_step = sem("dve_step")
        x_loaded = sem("x_loaded")
        handed_rows = sem("handed_rows")
        handed_prev = sem("handed_prev")
        handed = sem("handed")
        normed_up = sem("normed_up")
        xT_psum = sem("xT_psum")
        xT_up = sem("xT_up")
        gat_psum = sem("gat_psum")
        gat_h_up = sem("gat_h_up")
        edge_up = sem("edge_up")
        nmax_up = sem("nmax_up")
        edge_exp = sem("edge_exp")
        edge_T_psum = sem("edge_T_psum")
        edge_T_up = sem("edge_T_up")
        gat_out = sem("gat_out")
        elu_in = sem("elu_in")
        elu_up = sem("elu_up")
        logits_psum = sem("logits_psum")
        gap_up = sem("gap_up")
        gap_exp_up = sem("gap_exp_up")
        h1_psum = sem("h1_psum")
        h2_psum = sem("h2_psum")
        tanh_up = sem("tanh_up")
        hid_up = sem("hid_up")
        moe_psum = sem("moe_psum")
        moe_added = sem("moe_added")
        scores_psum = sem("scores_psum")
        scores_read = sem("scores_read")
        fin_up = sem("fin_up")
        fin_exp = sem("fin_exp")
        row_next_up = sem("row_next_up")
        diag_up = sem("diag_up")
        summed = sem("summed")
        kv_up = sem("kv_up")
        qk_psum = sem("qk_psum")
        qk_up = sem("qk_up")
        sim_psum = sem("sim_psum")
        sim_nmax_up = sem("sim_nmax_up")
        sim_exp = sem("sim_exp")
        prob_up = sem("prob_up")
        prob_T_psum = sem("prob_T_psum")
        prob_T_up = sem("prob_T_up")
        att_psum = sem("att_psum")
        att_up = sem("att_up")
        y_psum = sem("y_psum")
        y_up = sem("y_up")
        y_stored = sem("y_stored")

        def fetches(b, s):
            per_batch = STEPS // FETCH_SEMS
            return b * (16 * TOPK * per_batch) + 16 * TOPK * (s // FETCH_SEMS + 1)

        assert [s.num for s in sems] == list(range(sems[0].num, sems[0].num + len(sems)))

        def clear_semaphores():
            nc.sync.sem_clear(range(sems[0].num, sems[-1].num + 1))
            nc.all_engine_barrier(sem_only=True)

        pk_wt_sb = rows[0:DK, 0, :, :].rearrange("p a b -> p (a b)")[:, 0:2 * HEADS * D]
        pk_kt_sb = rows[0:DK, 0, :, :].rearrange("p a b -> p (a b)")[:, 2 * HEADS * D:4 * HEADS * D]
        adj_i = rows[:, 1, 0:2, :].bitcast(I32)
        gat_wt_sb = rows[:, 2, 0, :].rearrange("p (l e) -> p l e", l=2)
        gat_a_sb = rows[:, 2, 1, 0:4].rearrange("p (l e) -> p l e", l=2)

        setup_loads = [
            (const[:, :], consts), (gat_wt_sb, gat_wt), (gat_a_sb, gat_a), (gat_ext[:, :, 0:D], gat_w),
            (adj_i, adj.rearrange("(t p) j -> p t j", p=P)),
            (pk_wt_sb, pk_wt), (pk_kt_sb, pk_kt),
        ]
        weight_loads = [
            (gate_w_sb[:, :], gate_w), (gate_b_sb[:, :], gate_b),
            (w1_sb[:, :, :], w1.rearrange("e d h -> d e h")),
            (w2_sb[:, :, :], w2.rearrange("e d h -> d e h")),
            (w3_sb[:, :, :], w3.rearrange("e (c p) o -> p (e c) o", p=P)),
            (wq_sb[:, :], wq), (wo_sb[:, :, :], wo.rearrange("(h d) n -> d h n", d=D)),
        ]

        with nc.Block() as block:
            @block.sync
            def _(sp):
                for to, of in setup_loads:
                    sp.dma_start(to, of).then_inc(loaded, 16)
                sp.wait_ge(loaded, 16 * len(setup_loads))

            @block.tensor
            def _(pe):
                pe.wait_ge(loaded, 16 * len(setup_loads))
                for layer in range(2):
                    mm = nc.tensor.matmul(a0[:, 2 * layer:2 * layer + 2], gat_wt_sb[:, layer, :],
                                          gat_a_sb[:, layer, :], start=True, stop=True)
                mm.then_inc(ext_psum, 1)
                for n in range(2 * HEADS):
                    bank = (b0, b1)[n // 4 % 2]
                    if n % 4 == 0 and n >= 8:
                        pe.wait_ge(setup_mat_sb, n // 4 - 1)
                    mm = nc.tensor.matmul(bank[:, n % 4 * KEYS:(n % 4 + 1) * KEYS], pk_wt_sb[:, n * D:(n + 1) * D],
                                          pk_kt_sb[:, n * KEYS:(n + 1) * KEYS], start=True, stop=True)
                    if n % 4 == 3:
                        mm.then_inc(setup_mat, 1)

            @block.scalar
            def _(act):
                for c in range(2 * HEADS // 4):
                    act.wait_ge(setup_mat, c + 1)
                    nc.scalar.copy(pk_mat[:, 512 * c:512 * (c + 1)], (b0, b1)[c % 2][:, :]).then_inc(setup_mat_sb, 1)

            @block.vector
            def _(dve):
                dve.wait_ge(loaded, 16 * len(setup_loads))
                nc.vector.tensor_scalar(adj_bias[:, :, :], adj_i, 0.0, None, ALU.is_gt).then_inc(dve_step, 1)
                dve.wait_ge(dve_step, 1)
                nc.vector.tensor_scalar(adj_bias[:, :, :], adj_bias[:, :, :], 1.0, -NEG_BIG, ALU.subtract,
                                        ALU.mult)
                nc.vector.memset(gat_dst[:, :, :], 1.0).then_inc(dve_step, 1)
                dve.wait_ge(dve_step, 2)
                dve.wait_ge(ext_psum, 1)
                for layer in range(2):
                    nc.vector.tensor_copy(gat_ext[:, layer, D:D + 1], a0[:, 2 * layer:2 * layer + 1])
                    nc.vector.tensor_scalar(gat_dst[:, layer, :], gat_dst[:, layer, :],
                                            a0[:, 2 * layer + 1:2 * layer + 2], None, ALU.mult)
        clear_semaphores()

        STAGE = {"a": (0, res_a, xT_a, a0, a1), "b": (1, res_b, xT_b, b0, b1)}

        def plan_front(stage_a, stage_b):
            out = []
            if stage_b:
                out += [("norm", "b0"), ("norm_t", "b0"), ("gat_a", "b"), ("gat_b", "b"), ("gat_c", "b"),
                        ("norm", "b1"), ("norm_t", "b1"), ("scores", 0), ("scores", 1)]
            out += [("norm", "a0"), ("norm_t", "a0"), ("gat_a", "a")]
            out += [("keys", 0)] * stage_b
            out += [("gat_b", "a"), ("gat_c", "a"), ("norm", "a1"), ("norm_t", "a1")]
            out += [("scores", 2), ("keys", 1)] * stage_b
            out += [("gate", 0)]
            pieces = [
                [("scores", 3), ("keys", 2)], [("scores", 4), ("keys", 3), ("pairs", 0)],
                [("choose", (0, 0))], [("choose", (0, 4))], [("codes", 0), ("fin_exp", 0), ("rows", (0, 0))],
                [("rows", (0, 4)), ("weights", 0)],
                [("scores", 5), ("keys", 4)], [("scores", 6), ("keys", 5)], [("scores", 7), ("keys", 6)],
                [("keys", 7), ("pairs", 1)], [("choose", (1, 0))], [("choose", (1, 4))],
                [("codes", 1), ("fin_exp", 1)], [("rows", (1, 0))], [("rows", (1, 4))], [("weights", 1)],
            ]
            if not stage_b:
                out += [("up", 0)]
                for e in range(EXPERTS):
                    if e + 1 < EXPERTS:
                        out += [("up", e + 1)]
                    out += [("hid", e)]
                    if e:
                        out += [("add", e - 1)]
                    out += [("down", e)]
                return out + [("add", EXPERTS - 1)]
            for e in range(EXPERTS):
                out += [("up", e)] + pieces[e]
                if e:
                    out += [("add", e - 1)]
                out += [("hid", e), ("down", e)]
            return out + [("add", EXPERTS - 1)]

        def plan(s, stage_a, stage_b, gather, tail, attended):
            if s == 0:
                return (
                    [("norm", "b0")] * stage_b
                    + [("combine", STEPS - 2)] * tail
                    + [("norm_t", "b0"), ("gat_a", "b")] * stage_b
                    + [("diagonals", 0)] * gather
                    + [("combine", STEPS - 1)] * tail
                    + [("gat_b", "b")] * stage_b
                    + [("att_a", HEADS - 1)] * tail
                    + [("gat_c", "b")] * stage_b
                    + [("diagonals", 1), ("combine", 0)] * gather
                    + [("att_b", HEADS - 1)] * tail
                    + [("norm", "b1"), ("norm_t", "b1")] * stage_b
                    + [("last_rows", 0)] * gather
                )
            b_parts = {1: ([("scores", 0)], [("keys", 0)], []),
                       2: ([("scores", 1)], [("keys", 1)], []),
                       3: ([("scores", 2)], [("keys", 2)], []),
                       4: ([("scores", 3)], [("keys", 3), ("pairs", 0)], []),
                       5: ([], [("choose", (0, 0))], []),
                       6: ([], [("choose", (0, 4))], []),
                       7: ([("scores", 4)], [("codes", 0), ("rows", (0, 0)), ("rows", (0, 4))], []),
                       8: ([("fin_exp", 0)], [("weights", 0), ("keys", 4)], []),
                       9: ([("scores", 5)], [("keys", 5)], []),
                       10: ([("scores", 6)], [("keys", 6)], []),
                       11: ([("scores", 7)], [("keys", 7), ("pairs", 1)], []),
                       12: ([], [("choose", (1, 0))], []),
                       13: ([], [("choose", (1, 4))], []),
                       14: ([], [("codes", 1), ("fin_exp", 1), ("rows", (1, 0))], []),
                       15: ([], [("weights", 1), ("rows", (1, 4))], [])}
            a_parts = {1: ([], [("norm", "a0")], [("norm_t", "a0"), ("gat_a", "a")]),
                       2: ([("gat_b", "a")], [("gat_c", "a"), ("norm", "a1")], [("norm_t", "a1"), ("gate", 0)])}
            experts = {3: [0], 4: [1], 5: [2, 3], 6: [4], 7: [5], 8: [6, 7], 9: [8], 10: [9, 10], 11: [11],
                       12: [12, 13], 13: [14], 14: [15]}
            none = ([], [], [])
            b_before, b_beside, b_after = b_parts.get(s, none) if stage_b else none
            a_before, a_beside, a_after = a_parts.get(s, none) if stage_a else none
            mine = experts.get(s, []) if stage_a else []
            last = experts.get(s - 1, []) if stage_a else []
            out = []
            if s in attended and s % TILES == 1:
                out += [("att_norm", attended[s])]
            if last:
                out += [("add", last[0])]
            if len(last) > 1:
                out += [("hid", last[1]), ("down", last[1])]
            if mine:
                out += [("up", mine[0])]
            if s in attended:
                out += [("att_c" if s % TILES else "att_a", attended[s])]
            out += b_before + a_before
            if gather and s + 1 < STEPS:
                out += [("diagonals", s + 1)]
            if gather and s < STEPS - LATE:
                out += [("combine", s)]
            if s in attended and s % TILES == 0:
                out += [("att_b", attended[s])]
            out += b_beside + a_beside
            if len(last) > 1:
                out += [("add", last[1])]
            if mine:
                out += [("hid", mine[0]), ("down", mine[0])]
            if len(mine) > 1:
                out += [("up", mine[1])]
            if s in attended and attended[s] == HEADS - 1 and s % TILES == 1:
                out += [("project", 0)]
            out += b_after + a_after
            if mine and s == STEPS - 1:
                out += [("add", mine[0])]
            return out

        def run_pass(b, stage_a, stage_b, gather, tail):
            first_pass = stage_a and not stage_b
            up_banks = ((a0, a1),) if stage_b else ((a0, a1), (b0, b1))
            early = stage_b and not gather
            first = LATE if tail else 0

            def nth_sum(s):
                return s - (STEPS - LATE) if s >= STEPS - LATE else s + first

            attended = {s: (s // TILES - 1) % HEADS for s in range(STEPS)
                        if (tail if s < TILES else gather)}
            nth = {h: n for n, h in enumerate([HEADS - 1] * tail + list(range(HEADS - 1)) * gather)}
            if gather or tail:
                parts = [part for s in range(STEPS) for part in plan(s, stage_a, stage_b, gather, tail, attended)]
            else:
                parts = plan_front(stage_a, stage_b)
            nth_norm = {arg: n for n, arg in enumerate(arg for name, arg in parts if name == "norm")}
            nth_gat = {arg: n for n, arg in enumerate(arg for name, arg in parts if name == "gat_a")}

            with nc.Block(no_gpsimd_drain=True) as block:
                @block.sync
                def _(sp):
                    if stage_a:
                        if stage_b:
                            sp.wait_ge(handed, 1)
                        sp.dma_start(res_a[:, :, :], x[b + 2].rearrange("(t p) d -> p t d", p=P)).then_inc(x_loaded, 16)
                        if first_pass:
                            for to, of in weight_loads:
                                sp.dma_start(to, of).then_inc(weights_loaded, 16)
                        sp.wait_ge(x_loaded, 16)
                    if tail:
                        sp.wait_ge(y_up, 1)
                        sp.dma_start(out[b - 1].rearrange("(t p) d -> p t d", p=P), y_sb[:, :, :]).then_inc(y_stored, 16)
                        sp.wait_ge(y_stored, 16)

                @block.gpsimd
                def _(pool):
                    def fetch(s, row):
                        h, t = s // TILES, s % TILES
                        for k in range(TOPK):
                            pool.indirect_dma_start(
                                out=rows[:, s % SLOTS, k, :], out_offset=None, in_=table[:, :],
                                in_offset=bass.IndirectOffsetOnAxis(ap=row[:, t, h, k:k + 1], axis=0),
                            ).then_inc(fetched[s % FETCH_SEMS], 16)

                    if early:
                        pool.wait_ge(row_next_up, 1)
                        for s in EARLY:
                            fetch(s, row_next)
                    if not gather:
                        return
                    for s in range(STEPS):
                        if s in EARLY and not tail:
                            continue
                        if s == STEPS - TILES:
                            pool.wait_ge(handed_rows, 1)
                        n = s - SLOTS + first + 1
                        if n > 0:
                            pool.wait_ge(summed, n)
                        fetch(s, row)

                @block.scalar
                def _(act):
                    def norm(which):
                        _, _, xT, bank, _ = STAGE[which[0]]
                        act.wait_ge(xT_psum, nth_norm[which] + 1)
                        nc.scalar.copy(xT[:, :], bank[:, 0:TOKENS]).then_inc(xT_up, 1)

                    def gat_a(which):
                        n, (_, _, _, bank, bank_dst) = nth_gat[which], STAGE[which]
                        act.wait_ge(gat_psum, n + 1)
                        src = bank[:, :].rearrange("p (t c) -> p t c", t=TILES)[:, :, 0:D + 1]
                        nc.scalar.copy(gat_h[:, :, :], src).then_inc(gat_h_up, 1)
                        act.wait_ge(gat_h_up, n + 1)
                        for t in range(TILES):
                            ins = nc.scalar.activation(edge[:, t, :], bank_dst[:, 0:TOKENS], ACT.Identity,
                                                       bias=gat_h[:, t, D:D + 1])
                        ins.then_inc(edge_up, 1)

                    def gat_b(which):
                        n, bank = nth_gat[which], STAGE[which][4]
                        act.wait_ge(nmax_up, n + 1)
                        for t in range(TILES):
                            ins = nc.scalar.activation(edge[:, t, :], edge[:, t, :], ACT.Exp,
                                                       bias=edge_nmax[:, t:t + 1], accum_out=edge_sum[:, t:t + 1])
                        ins.then_inc(edge_exp, 1)
                        act.wait_ge(edge_T_psum, n + 1)
                        nc.scalar.copy(edge_T[:, :], bank[:, :]).then_inc(edge_T_up, 1)

                    def gat_c(which):
                        n = nth_gat[which]
                        act.wait_ge(elu_in, n + 1)
                        nc.scalar.activation(elu_exp, elu_neg, ACT.Exp).then_inc(elu_up, 1)

                    def gate(_):
                        act.wait_ge(gap_up, 1)
                        nc.scalar.activation(gap_exp[:, :], gap[:, :], ACT.Exp).then_inc(gap_exp_up, 1)

                    def up(e):
                        act.wait_ge(h1_psum, e + 1)
                        if e:
                            act.wait_ge(hid_up, e)
                        nc.scalar.activation(act_h[:, :], up_banks[e % len(up_banks)][0][:, :], ACT.Tanh, scale=0.5).then_inc(tanh_up, 1)

                    def weights(t):
                        act.wait_ge(fin_up, t + 1)
                        nc.scalar.activation(fin_e[:, :, :], fin_s[:, :, :], ACT.Exp).then_inc(fin_exp, 1)

                    def diagonals(s):
                        h, t = s // TILES, s % TILES
                        if s == 0:
                            act.wait_ge(handed, 1)
                        if s - 1 + first > 0:
                            act.wait_ge(summed, s - 1 + first)
                        for k in range(TOPK):
                            ins = nc.scalar.activation(diag[:, s % 2, k, :], ident, ACT.Copy,
                                                       scale=wt[:, t, h, k:k + 1])
                        ins.then_inc(diag_up, 1)

                    def keep_sums(s):
                        h, t = s // TILES, s % TILES
                        n = nth_sum(s)
                        if h >= 2 and s < STEPS - LATE:
                            act.wait_ge(att_psum, nth[h - 2] + 1)
                        if h == 1 and tail:
                            act.wait_ge(att_psum, nth[HEADS - 1] + 1)
                        act.wait_ge(summed, n + 1)
                        nc.scalar.copy(kv[:, h % 2, t, :], p_sum[:, 0:2 * D]).then_inc(kv_up, 1)

                    def attend_a(h):
                        n = nth[h]
                        act.wait_ge(qk_psum, n + 1)
                        nc.scalar.mul(qk_sb[:, 0:TOKENS], p_qk[:, 0:TOKENS], float(D) ** -0.5)
                        nc.scalar.copy(qk_sb[:, TOKENS:], p_qk[:, TOKENS:]).then_inc(qk_up, 1)

                    def attend_b(h):
                        n = nth[h]
                        act.wait_ge(sim_nmax_up, n + 1)
                        nc.scalar.activation(prob[:, 0:P], sim[:, 0:P], ACT.Exp, bias=sim_nmax[:, 0:1],
                                             accum_out=sim_sum[:, 0:1])
                        nc.scalar.activation(prob[:, P:], sim[:, P:], ACT.Exp, bias=sim_nmax[:, 1:2],
                                             accum_out=sim_sum[:, 1:2]).then_inc(sim_exp, 1)

                    def attend_c(h):
                        n = nth[h]
                        act.wait_ge(prob_T_psum, n + 1)
                        nc.scalar.copy(prob_T[:, :], p_sim[:, 0:3 * P]).then_inc(prob_T_up, 1)
                        act.wait_ge(att_psum, n + 1)
                        nc.scalar.copy(att_T[:, h, :], p_qk[:, 0:TOKENS]).then_inc(att_up, 1)

                    run = {"norm_t": norm, "gat_a": gat_a, "gat_b": gat_b, "gat_c": gat_c, "gate": gate, "up": up,
                           "fin_exp": weights, "diagonals": diagonals, "combine": keep_sums,
                           "att_a": attend_a, "att_b": attend_b, "att_c": attend_c}
                    for name, arg in parts:
                        if name in run:
                            run[name](arg)

                @block.tensor
                def _(pe):
                    def norm(which):
                        bank = STAGE[which[0]][3]
                        pe.wait_ge(normed_up, nth_norm[which] + 1)
                        for t in range(TILES):
                            mm = nc.tensor.transpose(bank[:, t * P:(t + 1) * P], normed[:, t, :], ident)
                        mm.then_inc(xT_psum, 1)

                    def gat_a(which):
                        layer, _, xT, bank, bank_dst = STAGE[which]
                        pe.wait_ge(xT_up, nth_norm[which + "0"] + 1)
                        nc.tensor.matmul(bank_dst[:, 0:TOKENS], gat_dst[:, layer, :], xT[:, :], start=True, stop=True)
                        for t in range(TILES):
                            mm = nc.tensor.matmul(bank[:, t * 256:t * 256 + D + 1], xT[:, t * P:(t + 1) * P],
                                                  gat_ext[:, layer, :], start=True, stop=True)
                        mm.then_inc(gat_psum, 1)

                    def gat_b(which):
                        n, (_, _, _, bank, bank_T) = nth_gat[which], STAGE[which]
                        pe.wait_ge(edge_exp, n + 1)
                        for t in range(TILES):
                            for j in range(TILES):
                                mm = nc.tensor.transpose(bank_T[:, j * TOKENS + t * P:j * TOKENS + (t + 1) * P],
                                                         edge[:, t, j * P:(j + 1) * P], ident)
                        mm.then_inc(edge_T_psum, 1)
                        pe.wait_ge(edge_T_up, n + 1)
                        for t in range(TILES):
                            for j in range(TILES):
                                mm = nc.tensor.matmul(bank[:, t * P:(t + 1) * P],
                                                      edge_T[:, j * TOKENS + t * P:j * TOKENS + (t + 1) * P],
                                                      gat_h[:, j, 0:D], start=(j == 0), stop=(j == TILES - 1))
                        mm.then_inc(gat_out, 1)

                    def gate(_):
                        if first_pass:
                            pe.wait_ge(weights_loaded, 16 * len(weight_loads))
                        pe.wait_ge(xT_up, nth_norm["a1"] + 1)
                        for t in range(TILES):
                            mm = nc.tensor.matmul(a1[:, t * EXPERTS:(t + 1) * EXPERTS], xT_a[:, t * P:(t + 1) * P],
                                                  gate_w_sb[:, :], start=True, stop=True)
                        mm.then_inc(logits_psum, 1)

                    def up(e):
                        if e == 0:
                            pe.wait_ge(gap_up, 1)
                        elif e >= len(up_banks):
                            pe.wait_ge(hid_up, e - len(up_banks) + 1)
                        bank_h1, bank_h2 = up_banks[e % len(up_banks)]
                        for w, bank, signal in ((w1_sb, bank_h1, h1_psum), (w2_sb, bank_h2, h2_psum)):
                            for c in range(CHUNKS):
                                mm = nc.tensor.matmul(bank[:, c * TOKENS:(c + 1) * TOKENS],
                                                      w[:, e, c * P:(c + 1) * P], xT_a[:, :], start=True, stop=True)
                            mm.then_inc(signal, 1)

                    def down(e):
                        pe.wait_ge(hid_up, e + 1)
                        if e:
                            pe.wait_ge(moe_added, e)
                        for t in range(TILES):
                            for c in range(CHUNKS):
                                mm = nc.tensor.matmul(a2[:, t * P:(t + 1) * P], hid[:, e % 2, c, t * P:(t + 1) * P],
                                                      w3_sb[:, CHUNKS * e + c, :], start=(c == 0),
                                                      stop=(c == CHUNKS - 1))
                        mm.then_inc(moe_psum, 1)

                    def keys(n):
                        t, c = n // 4, n % 4
                        pe.wait_ge(xT_up, nth_norm["b1"] + 1)
                        if n >= 2:
                            pe.wait_ge(scores_read, n - 1)
                        nc.tensor.matmul((b0, b1)[n % 2][:, :], xT_b[:, t * P:(t + 1) * P],
                                         pk_mat[:, c * 512:(c + 1) * 512], start=True,
                                         stop=True).then_inc(scores_psum, 1)

                    def combine(s):
                        n = nth_sum(s)
                        if n:
                            pe.wait_ge(kv_up, n)
                        if s < STEPS - LATE:
                            pe.wait_ge(diag_up, s + 1)
                        batch = b if s < STEPS - LATE else b - 1
                        pe.wait_ge(fetched[s % FETCH_SEMS], fetches(batch, s))
                        for k in range(TOPK):
                            mm = nc.tensor.matmul(p_sum[:, 0:2 * D], diag[:, s % 2, k, :], rows[:, s % SLOTS, k, :],
                                                  start=(k == 0), stop=(k == TOPK - 1))
                        mm.then_inc(summed, 1)

                    def attend_a(h):
                        n = nth[h]
                        if h == 0:
                            pe.wait_ge(handed, 1)
                            if tail:
                                pe.wait_ge(y_up, 1)
                        pe.wait_ge(kv_up, nth_sum(TILES * h + 1) + 1)
                        if n >= 1:
                            pe.wait_ge(att_up, n)
                        if h == HEADS - 1:
                            pe.wait_ge(handed_prev, 1)
                        rhs = xT_prev if h == HEADS - 1 else xT_cur
                        nc.tensor.matmul(p_qk[:, 0:TOKENS], wq_sb[:, h * D:(h + 1) * D], rhs[:, :],
                                         start=True, stop=True)
                        for t in range(TILES):
                            mm = nc.tensor.transpose(p_qk[:, TOKENS + t * P:TOKENS + (t + 1) * P],
                                                     kv[:, h % 2, t, 0:D], ident)
                        mm.then_inc(qk_psum, 1)
                        pe.wait_ge(qk_up, n + 1)
                        nc.tensor.matmul(p_sim[:, 0:P], qk_sb[:, 0:P], qk_sb[:, TOKENS:TOKENS + P], start=True,
                                         stop=True)
                        nc.tensor.matmul(p_sim[:, P:3 * P], qk_sb[:, P:2 * P], qk_sb[:, TOKENS:], start=True,
                                         stop=True).then_inc(sim_psum, 1)

                    def attend_c(h):
                        n = nth[h]
                        pe.wait_ge(prob_up, n + 1)
                        for c in range(3):
                            mm = nc.tensor.transpose(p_sim[:, c * P:(c + 1) * P], prob[:, c * P:(c + 1) * P], ident)
                        mm.then_inc(prob_T_psum, 1)
                        pe.wait_ge(prob_T_up, n + 1)
                        nc.tensor.matmul(p_qk[:, 0:TOKENS], kv[:, h % 2, 0, D:], prob_T[:, 0:TOKENS], start=True,
                                         stop=False)
                        nc.tensor.matmul(p_qk[:, P:TOKENS], kv[:, h % 2, 1, D:], prob_T[:, TOKENS:], start=False,
                                         stop=True).then_inc(att_psum, 1)

                    def project(_):
                        pe.wait_ge(att_up, 1)
                        for t in range(TILES):
                            for h in range(HEADS):
                                mm = nc.tensor.matmul(p_sim[:, t * P:(t + 1) * P], att_T[:, h, t * P:(t + 1) * P],
                                                      wo_sb[:, h, :], start=(h == 0), stop=(h == HEADS - 1))
                        mm.then_inc(y_psum, 1)

                    run = {"norm_t": norm, "gat_a": gat_a, "gat_b": gat_b, "gate": gate, "up": up, "down": down,
                           "scores": keys, "combine": combine, "att_a": attend_a, "att_c": attend_c,
                           "project": project}
                    for name, arg in parts:
                        if name in run:
                            run[name](arg)

                @block.vector
                def _(dve):
                    chain = [0]

                    def link(ins):
                        chain[0] += 1
                        ins.then_inc(dve_step, 1)
                        dve.wait_ge(dve_step, chain[0])

                    def step(ins):
                        chain[0] += 1
                        ins.then_inc(dve_step, 1)
                        return chain[0]

                    v = nc.vector

                    def norm(which):
                        res = STAGE[which[0]][1]
                        if which == "a0":
                            dve.wait_ge(x_loaded, 16)
                        for t in range(TILES):
                            last = step(v.bn_stats(stats[:, t, :], res[:, t, :]))
                        dve.wait_ge(dve_step, last)
                        for t in range(TILES):
                            last = step(v.bn_aggr(meanvar[:, t, :], stats[:, t, :]))
                        dve.wait_ge(dve_step, last)
                        link(v.tensor_scalar(var_eps[:, :], meanvar[:, :, 1], EPS, None, ALU.add))
                        link(v.tensor_scalar(rs_i[:, :], var_eps[:, :].bitcast(I32), 1, None,
                                             ALU.logical_shift_right))
                        link(v.tensor_scalar(rs_y[:, :].bitcast(I32), rs_i[:, :], -1.0, float(RSQRT_MAGIC), ALU.mult,
                                             ALU.add))
                        for _ in range(3):
                            link(v.tensor_tensor(rs_t[:, :], rs_y[:, :], rs_y[:, :], ALU.mult))
                            link(v.scalar_tensor_tensor(out=rs_t[:, :], in0=rs_t[:, :], scalar=-0.5,
                                                        in1=var_eps[:, :], op0=ALU.mult, op1=ALU.mult))
                            link(v.scalar_tensor_tensor(out=rs_y[:, :], in0=rs_t[:, :], scalar=1.5, in1=rs_y[:, :],
                                                        op0=ALU.add, op1=ALU.mult))
                        if nth_norm[which]:
                            dve.wait_ge(xT_psum, nth_norm[which])
                        for t in range(TILES):
                            ins = v.tensor_scalar(normed[:, t, :], res[:, t, :], meanvar[:, t, 0:1],
                                                  rs_y[:, t:t + 1], ALU.subtract, ALU.mult)
                        ins.then_inc(normed_up, 1)

                    def gat_a(which):
                        n = nth_gat[which]
                        dve.wait_ge(edge_up, n + 1)
                        for t in range(TILES):
                            last = step(v.scalar_tensor_tensor(out=edge[:, t, :], in0=edge[:, t, :], scalar=SLOPE,
                                                               in1=edge[:, t, :], op0=ALU.mult, op1=ALU.max))
                        dve.wait_ge(dve_step, last)
                        for t in range(TILES):
                            last = step(v.tensor_tensor_reduce(edge[:, t, :], edge[:, t, :], adj_bias[:, t, :], 1.0,
                                                               LOWEST, ALU.add, ALU.max, edge_max[:, t:t + 1]))
                        dve.wait_ge(dve_step, last)
                        v.tensor_scalar(edge_nmax[:, :], edge_max[:, :], -1.0, None, ALU.mult).then_inc(nmax_up, 1)

                    def gat_b(which):
                        dve.wait_ge(edge_exp, nth_gat[which] + 1)
                        link(v.reciprocal(edge_inv[:, :], edge_sum[:, :]))

                    def gat_c(which):
                        n, (_, res, _, bank, _) = nth_gat[which], STAGE[which]
                        dve.wait_ge(gat_out, n + 1)
                        for t in range(TILES):
                            ins = v.tensor_scalar(elu_neg[:, t, :], bank[:, t * P:(t + 1) * P], edge_inv[:, t:t + 1],
                                                  0.0, ALU.mult, ALU.min)
                        ins.then_inc(elu_in, 1)
                        for t in range(TILES):
                            last = step(v.tensor_scalar(elu_pos[:, t, :], bank[:, t * P:(t + 1) * P],
                                                        edge_inv[:, t:t + 1], 0.0, ALU.mult, ALU.max))
                        dve.wait_ge(dve_step, last)
                        dve.wait_ge(elu_up, n + 1)
                        link(v.scalar_tensor_tensor(out=elu_pos[:, :, :], in0=elu_exp[:, :, :], scalar=-1.0,
                                                    in1=elu_pos[:, :, :], op0=ALU.add, op1=ALU.add))
                        link(v.tensor_tensor(res[:, :, :], res[:, :, :], elu_pos[:, :, :], ALU.add))

                    def gate(_):
                        dve.wait_ge(logits_psum, 1)
                        for t in range(TILES):
                            last = step(v.tensor_tensor(logits[:, t, :], a1[:, t * EXPERTS:(t + 1) * EXPERTS],
                                                        gate_b_sb[:, :], ALU.add))
                        dve.wait_ge(dve_step, last)
                        for t in range(TILES):
                            last = step(v.max(best[:, t, :], logits[:, t, :]))
                        dve.wait_ge(dve_step, last)
                        v.tensor_tensor(gap[:, :], best[:, :, 1], best[:, :, 0], ALU.subtract).then_inc(gap_up, 1)
                        for t in range(TILES):
                            last = step(v.max_index(best_i[:, t, :], best[:, t, :], logits[:, t, :]))
                        dve.wait_ge(dve_step, last)
                        link(v.tensor_copy(best_f[:, :, :], best_i[:, :, 0:2]))
                        dve.wait_ge(gap_exp_up, 1)
                        link(v.tensor_scalar(gate_den[:, :], gap_exp[:, :], 1.0, None, ALU.add))
                        link(v.reciprocal(gate_p[:, :, 0], gate_den[:, :]))
                        link(v.tensor_tensor(gate_p[:, :, 1], gate_p[:, :, 0], gap_exp[:, :], ALU.mult))
                        for t in range(TILES):
                            for k in range(2):
                                last = step(v.tensor_scalar(disp[:, t, k, :], iota[:, 0:EXPERTS],
                                                            best_f[:, t, k:k + 1], gate_p[:, t, k:k + 1],
                                                            ALU.is_equal, ALU.mult))
                        dve.wait_ge(dve_step, last)
                        link(v.tensor_tensor(dispatch[:, :, :], disp[:, :, 0, :], disp[:, :, 1, :], ALU.add))

                    def hidden(e):
                        bank_h1, bank_h2 = up_banks[e % len(up_banks)]
                        dve.wait_ge(tanh_up, e + 1)
                        link(v.scalar_tensor_tensor(out=act_h[:, :], in0=act_h[:, :], scalar=1.0, in1=bank_h1[:, :],
                                                    op0=ALU.add, op1=ALU.mult))
                        dve.wait_ge(h2_psum, e + 1)
                        if e >= 2:
                            dve.wait_ge(moe_psum, e - 1)
                        v.scalar_tensor_tensor(out=hid[:, e % 2, :, :].rearrange("p c n -> p (c n)"),
                                               in0=act_h[:, :], scalar=0.5, in1=bank_h2[:, :], op0=ALU.mult,
                                               op1=ALU.mult).then_inc(hid_up, 1)

                    def add(e):
                        dve.wait_ge(moe_psum, e + 1)
                        if e:
                            dve.wait_ge(moe_added, e)
                        for t in range(TILES):
                            ins = v.scalar_tensor_tensor(out=res_a[:, t, :], in0=a2[:, t * P:(t + 1) * P],
                                                         scalar=dispatch[:, t, e:e + 1], in1=res_a[:, t, :],
                                                         op0=ALU.mult, op1=ALU.add)
                        ins.then_inc(moe_added, 1)

                    def top16(best_out, index_out, rest_of, scores):
                        n = range(len(scores))
                        for i in n:
                            last = step(v.max(best_out[i][:, 0:8], scores[i]))
                        dve.wait_ge(dve_step, last)
                        for i in n:
                            last = step(v.match_replace(rest_of[i], best_out[i][:, 0:8], scores[i], LOWEST))
                        for i in n:
                            step(v.max_index(index_out[i][:, 0:8], best_out[i][:, 0:8], scores[i]))
                        dve.wait_ge(dve_step, last)
                        for i in n:
                            last = step(v.max(best_out[i][:, 8:16], rest_of[i]))
                        dve.wait_ge(dve_step, last)
                        for i in n:
                            last = step(v.max_index(index_out[i][:, 8:16], best_out[i][:, 8:16], rest_of[i]))
                        return last

                    def keys(n):
                        bank = (b0, b1)[n % 2]
                        dve.wait_ge(scores_psum, n + 1)
                        for i in range(2):
                            h = n % 4 * 2 + i
                            last = top16([sc[:, h, p, :] for p in range(2)], [ix[:, h, p, :] for p in range(2)],
                                         [rest[:, p, :] for p in range(2)],
                                         [bank[:, (2 * i + p) * KEYS:(2 * i + p + 1) * KEYS] for p in range(2)])
                            dve.wait_ge(dve_step, last)
                        v.engine_nop().then_inc(scores_read, 1)

                    def pairs(t):
                        link(v.tensor_copy(ixf[:, :, :, :], ix[:, :, :, :]))
                        link(v.tensor_scalar(ixf[:, :, 1, :], ixf[:, :, 1, :], float(KEYS), None, ALU.mult))
                        for src, dst in ((sc, pair_s), (ixf, pair_i)):
                            for i in range(SINGLES):
                                w = PAIR_ROWS[i]
                                last = step(v.tensor_tensor(dst[:, :, PAIR_AT[i]:PAIR_AT[i] + w],
                                                            src[:, :, 1, 0:w],
                                                            src[:, :, 0, i:i + 1].to_broadcast([P, HEADS, w]),
                                                            ALU.add))
                            last = step(v.tensor_tensor(dst[:, :, PAIR_AT[SINGLES]:], src[:, :, 0, SINGLES:],
                                                        src[:, :, 1, 0:1].to_broadcast([P, HEADS, TOPK - SINGLES]),
                                                        ALU.add))
                        dve.wait_ge(dve_step, last)
                        link(v.tensor_tensor(pair_i[:, :, :], pair_i[:, :, :],
                                             pair_code.unsqueeze(1).to_broadcast([P, HEADS, PAIRS]), ALU.add))

                    def choose(which):
                        t, h0 = which
                        n, hs = range(4), range(h0, h0 + 4)
                        last = top16([fin_s[:, h, :] for h in hs], [fin_p[:, h, :] for h in hs],
                                     [rest2[:, i, :] for i in n], [pair_s[:, h, :] for h in hs])
                        dve.wait_ge(dve_step, last)
                        for i, h in zip(n, hs):
                            last = step(v.match_replace(rest2[:, i, :], fin_s[:, h, 8:16], rest2[:, i, :], LOWEST))
                        dve.wait_ge(dve_step, last)
                        link(v.scalar_tensor_tensor(out=chosen[:, :, :], in0=rest2[:, :, :], scalar=LOWEST,
                                                    in1=pair_i[:, h0:h0 + 4, :], op0=ALU.is_equal, op1=ALU.mult))
                        for i, h in zip(n, hs):
                            last = step(v.max(code[:, h, 0:8], chosen[:, i, :]))
                        dve.wait_ge(dve_step, last)
                        for i, h in zip(n, hs):
                            last = step(v.match_replace(chosen[:, i, :], code[:, h, 0:8], chosen[:, i, :], -1.0))
                        dve.wait_ge(dve_step, last)
                        for i, h in zip(n, hs):
                            last = step(v.max(code[:, h, 8:16], chosen[:, i, :]))
                        dve.wait_ge(dve_step, last)

                    def codes(t):
                        step(v.tensor_copy(fin_sum[:, :], fin_s[:, :, 0]))
                        step(v.tensor_copy(fin_pf[:, :, :], fin_p[:, :, :]))
                        link(v.tensor_copy(code_i[:, :, :], code[:, :, :]))
                        link(v.tensor_scalar(code_i[:, :, :], code_i[:, :, :], 14, None, ALU.logical_shift_right))
                        v.tensor_tensor(fin_s[:, :, :], fin_s[:, :, :],
                                        fin_sum[:, :].unsqueeze(2).to_broadcast([P, HEADS, TOPK]),
                                        ALU.subtract).then_inc(fin_up, 1)
                        link(v.tensor_copy(code_p[:, :, :], code_i[:, :, :]))
                        link(v.scalar_tensor_tensor(out=code[:, :, :], in0=code_p[:, :, :], scalar=-float(KEYS * KEYS),
                                                    in1=code[:, :, :], op0=ALU.mult, op1=ALU.add))

                    def table_rows(which):
                        t, h0 = which
                        hs = slice(h0, h0 + 4)
                        shape = [P, 4, TOPK, TOPK]
                        link(v.tensor_tensor(hit[:, :, :, :], code_p[:, hs, :].unsqueeze(2).to_broadcast(shape),
                                             fin_pf[:, hs, :].unsqueeze(3).to_broadcast(shape), ALU.is_equal))
                        link(v.tensor_tensor(hit[:, :, :, :], hit[:, :, :, :],
                                             code[:, hs, :].unsqueeze(2).to_broadcast(shape), ALU.mult))
                        link(v.tensor_reduce(fin_i[:, hs, :], hit[:, :, :, :], AX.X, ALU.add))
                        if h0:
                            ins = v.tensor_tensor(row_next[:, t, :, :], fin_i[:, :, :],
                                                  head_row.rearrange("p (h k) -> p h k", h=HEADS), ALU.add)
                            if early and t == 0:
                                ins.then_inc(row_next_up, 1)
                            else:
                                link(ins)

                    def weights(t):
                        dve.wait_ge(fin_exp, t + 1)
                        link(v.tensor_reduce(fin_sum[:, :], fin_e[:, :, :], AX.X, ALU.add))
                        link(v.reciprocal(fin_sum[:, :], fin_sum[:, :]))
                        link(v.tensor_tensor(wt_next[:, t, :, :], fin_e[:, :, :],
                                             fin_sum[:, :].unsqueeze(2).to_broadcast([P, HEADS, TOPK]), ALU.mult))

                    def attend_max(h):
                        n = nth[h]
                        dve.wait_ge(sim_psum, n + 1)
                        step(v.tensor_tensor_reduce(sim[:, 0:P], p_sim[:, 0:P], causal[:, P:], 1.0, LOWEST, ALU.add,
                                                    ALU.max, sim_max[:, 0:1]))
                        link(v.tensor_tensor_reduce(sim[:, P:], p_sim[:, P:3 * P], causal, 1.0, LOWEST, ALU.add,
                                                    ALU.max, sim_max[:, 1:2]))
                        v.tensor_scalar(sim_nmax[:, :], sim_max[:, :], -1.0, None, ALU.mult).then_inc(sim_nmax_up, 1)

                    def attend_norm(h):
                        n = nth[h]
                        dve.wait_ge(sim_exp, n + 1)
                        link(v.reciprocal(sim_inv[:, :], sim_sum[:, :]))
                        v.tensor_scalar(prob[:, 0:P], prob[:, 0:P], sim_inv[:, 0:1], None, ALU.mult)
                        v.tensor_scalar(prob[:, P:], prob[:, P:], sim_inv[:, 1:2], None, ALU.mult).then_inc(prob_up, 1)

                    def last_rows(_):
                        if tail:
                            for s in range(STEPS - TILES, STEPS):
                                dve.wait_ge(fetched[s % FETCH_SEMS], fetches(b - 1, s))
                        v.tensor_copy(row[:, :, HEADS - 1, :], row_next[:, :, HEADS - 1, :]).then_inc(handed_rows, 1)
                        dve.wait_ge(handed_rows, 1)

                    def project(_):
                        dve.wait_ge(y_psum, 1)
                        v.tensor_tensor(y_sb[:, :, :], p_sim[:, 0:TOKENS].rearrange("p (t d) -> p t d", t=TILES),
                                        res_prev[:, :, :], ALU.add).then_inc(y_up, 1)

                    run = {"norm": norm, "gat_a": gat_a, "gat_b": gat_b, "gat_c": gat_c, "gate": gate,
                           "hid": hidden, "add": add, "keys": keys, "pairs": pairs, "choose": choose,
                           "codes": codes, "rows": table_rows,
                           "weights": weights, "att_b": attend_max, "att_norm": attend_norm,
                           "last_rows": last_rows, "project": project}
                    if tail:
                        v.tensor_copy(xT_prev[:, :], xT_cur[:, :])
                        v.tensor_copy(res_prev[:, :, :], res_cur[:, :, :]).then_inc(handed_prev, 1)
                        dve.wait_ge(handed_prev, 1)
                    if gather:
                        v.tensor_copy(xT_cur[:, :], xT_b[:, :])
                        link(v.tensor_copy(res_cur[:, :, :], res_b[:, :, :]))
                        last = v.tensor_copy(wt[:, :, :, :], wt_next[:, :, :, :])
                    if stage_b:
                        last = v.tensor_copy(res_b[:, :, :], res_a[:, :, :])
                    if gather or stage_b:
                        last.then_inc(handed, 1)
                        dve.wait_ge(handed, 1)
                    for name, arg in parts:
                        if name in run:
                            run[name](arg)
                    if early:
                        for s in EARLY:
                            dve.wait_ge(fetched[s % FETCH_SEMS], fetches(0, s))
                        dve.wait_ge(row_next_up, 1)
                    if stage_b:
                        if gather:
                            for s in range(STEPS - TILES - FETCH_SEMS, STEPS - TILES):
                                dve.wait_ge(fetched[s % FETCH_SEMS], fetches(b, s))
                        v.tensor_copy(row[:, :, 0:HEADS - 1, :], row_next[:, :, 0:HEADS - 1, :])
            clear_semaphores()

        run_pass(-2, stage_a=True, stage_b=False, gather=False, tail=False)
        run_pass(-1, stage_a=True, stage_b=True, gather=False, tail=False)
        run_pass(0, stage_a=True, stage_b=True, gather=True, tail=False)
        with nc.Fori(1, BATCHES - 2) as b:
            run_pass(b, stage_a=True, stage_b=True, gather=True, tail=True)
        run_pass(BATCHES - 2, stage_a=False, stage_b=True, gather=True, tail=True)
        run_pass(BATCHES - 1, stage_a=False, stage_b=False, gather=True, tail=True)
        run_pass(BATCHES, stage_a=False, stage_b=False, gather=False, tail=True)


def kernel(**inputs):
    import concourse.bacc as _bacc
    from concourse.bass_utils import run_bass_kernel_spmd as _run

    a = {k: np.asarray(v) for k, v in inputs.items()}
    nc = _bacc.Bacc("TRN2", target_bir_lowering=False, num_devices=1)
    arrays = {
        "x": a["x"],
        "adj": a["adj"],
        "consts": shape_constants(),
        "gat_w": np.stack([a["L0_gnn_W"], a["L1_gnn_W"]], axis=1),
        "gat_wt": np.stack([a["L0_gnn_W"].T, a["L1_gnn_W"].T], axis=1),
        "gat_a": np.stack([a["L0_gnn_a"].reshape(2, D).T, a["L1_gnn_a"].reshape(2, D).T], axis=1),
        "gate_w": a["L0_ffn_gate_w"],
        "gate_b": np.broadcast_to(a["L0_ffn_gate_b"][None, :], (P, EXPERTS)),
        "w1": a["L0_ffn_w1"],
        "w2": a["L0_ffn_w2"],
        "w3": a["L0_ffn_w3"],
        "pk_wt": a["L1_ffn_Wq_pk"].reshape(D, 2, HEADS, DK).transpose(3, 2, 1, 0).reshape(DK, 2 * HEADS * D),
        "pk_kt": a["L1_ffn_pk_keys"].transpose(3, 2, 0, 1).reshape(DK, 2 * HEADS * KEYS),
        "wq": a["L1_ffn_Wq"],
        "table": np.concatenate([a["L1_ffn_keys_table"], a["L1_ffn_values_table"]], axis=1),
        "wo": a["L1_ffn_Wo"],
    }
    arrays = {f"in_{k}_dram": np.ascontiguousarray(v) for k, v in arrays.items()}
    args = [nc.dram_tensor(k, v.shape, mybir.dt.from_np(v.dtype), kind="ExternalInput").ap()
            for k, v in arrays.items()]
    args.append(nc.dram_tensor("out_0_dram", a["x"].shape, F32, kind="ExternalOutput").ap())
    build(nc, *args)
    r = _run(nc, [arrays], core_ids=[0])
    return r.results[0]["out_0_dram"]
```
